# Optimizing a Trainium2 kernel written in Bass

```python
import numpy as np
import jax
import jax.numpy as jnp

def _softmax(x, axis=-1):
    return jax.nn.softmax(x, axis=axis)

def _gelu(x):
    return jax.nn.gelu(x, approximate=True)

def _silu(x):
    return jax.nn.silu(x)

def _sigmoid(x):
    return jax.nn.sigmoid(x)

def _layernorm(x, axis=-1, eps=1e-05):
    m = jnp.mean(x, axis=axis, keepdims=True)
    v = jnp.var(x, axis=axis, keepdims=True)
    return (x - m) / jnp.sqrt(v + eps)

def _scatter_add(tgt, idx, src, axis=0):
    return tgt.at[idx].add(src)

def _segment_sum(src, seg, n):
    return jax.ops.segment_sum(src, seg, n)
kernel_name = 'mk_xattn_ffn_d1_seqx_r4_1a51a3'

def setup_inputs(seed: int=0):
    np.random.seed(seed)
    _w = jnp.asarray

    def _rec_inputs():
        import jax
        import jax.numpy as jnp
        _rk = jax.random.key(seed)
        x = 7.22e-05 + 1 * jax.random.normal(jax.random.fold_in(_rk, 1), (4, 512, 512), jnp.float32)
        _lenS = 512 - jax.random.randint(jax.random.fold_in(_rk, 7), (4,), 0, max(1, 512 // 4) + 1, jnp.int32)
        _lenS2 = 512 - jax.random.randint(jax.random.fold_in(_rk, 8), (4,), 0, max(1, 512 // 4) + 1, jnp.int32)
        _ctx_2048P = jax.random.normal(jax.random.fold_in(_rk, 11), (4, 16, 512), jnp.float32)
        _ctx_2048c = jax.random.dirichlet(jax.random.fold_in(_rk, 511), 0.3 * jnp.ones((16,), jnp.float32), (4, 512))
        _ctx_2048t = jnp.einsum('bsk,bkd->bsd', _ctx_2048c, _ctx_2048P)
        _ctx_2048t = _ctx_2048t * jax.lax.rsqrt(jnp.mean(jnp.square(_ctx_2048t)) + 1e-12) * 0.953939
        ctx_2048 = 4.13588e-05 + 0.999923 * (_ctx_2048t + 0.3 * jax.random.normal(jax.random.fold_in(_rk, 611), (4, 512, 512), jnp.float32))
        return (x, ctx_2048)
    x, ctx_2048 = _rec_inputs()

    def _L0_xattn_setup():
        import jax, jax.numpy as jnp
        import numpy as np
        B, S, DIM, HD = (4, 256, 512, 128)
        H = DIM // HD
        GN_EPS = 0.001

        def _decay_masks(n_heads, seq_len):
            gam = 1.0 - 2.0 ** (-5.0 - jnp.arange(n_heads, dtype=jnp.float32))
            idx = jnp.arange(seq_len, dtype=jnp.float32)
            expo = idx[None, :] - idx[:, None]
            D = jnp.where(expo[None, :, :] <= 0, gam[:, None, None] ** expo[None, :, :], 0.0)
            return D / jnp.sqrt(D.sum(axis=-1))[:, None, :]
        key = jax.random.key(seed)
        ks = jax.random.split(key, 8)
        x = jax.random.normal(ks[0], (B, S, DIM), dtype=jnp.float32)
        k = jax.random.normal(ks[1], (B, S, DIM), dtype=jnp.float32)
        v = jax.random.normal(ks[2], (B, S, DIM), dtype=jnp.float32)
        Wh = jax.random.normal(ks[3], (H, HD, HD), dtype=jnp.float32) / np.sqrt(HD)
        wg_w = jax.random.normal(ks[4], (DIM, DIM), dtype=jnp.float32) / np.sqrt(DIM)
        wo_w = jax.random.normal(ks[5], (DIM, DIM), dtype=jnp.float32) / np.sqrt(DIM)
        gn_gamma = jnp.ones((DIM,), dtype=jnp.float32)
        gn_beta = jnp.zeros((DIM,), dtype=jnp.float32)
        return {'x': x, 'k': k, 'v': v, 'Wh': Wh, 'wg_w': wg_w, 'wo_w': wo_w, 'gn_gamma': gn_gamma, 'gn_beta': gn_beta}
    _L0_xattn_all = _L0_xattn_setup()
    _L0_xattn_in = {k: v for k, v in _L0_xattn_all.items() if k in ('Wh', 'wg_w', 'wo_w', 'gn_gamma', 'gn_beta')}
    del _L0_xattn_all

    def _L0_ffn_setup():
        import jax, jax.numpy as jnp
        import numpy as np
        DIM = 512
        INTER = 352
        E = 16
        TOPK = 4
        G = 4
        TOPK_G = 2
        N_SHARED = 2
        SHARED_INTER = N_SHARED * INTER
        ROUTE_SCALE = 1.0

        def _moe_forward(x, Wg, W1, W3, W2, Ws1, Ws3, Ws2):
            B, S, D = x.shape
            xt = x.reshape(-1, D)
            T = xt.shape[0]
            scores = jax.nn.softmax(xt @ Wg.T, axis=-1)
            sg = scores.reshape(T, G, E // G)
            group_scores = sg.max(axis=-1)
            gidx = jax.lax.top_k(group_scores, TOPK_G)[1]
            gmask = jax.nn.one_hot(gidx, G, dtype=jnp.float32).sum(axis=1) > 0
            masked = jnp.where(gmask[:, :, None], sg, -jnp.inf).reshape(T, E)
            topi = jax.lax.top_k(masked, TOPK)[1]
            weights = jnp.take_along_axis(scores, topi, axis=1) * ROUTE_SCALE
            combine = jnp.zeros((T, E), xt.dtype).at[jnp.arange(T)[:, None], topi].add(weights)
            h = jax.nn.silu(jnp.einsum('td,eid->eti', xt, W1)) * jnp.einsum('td,eid->eti', xt, W3)
            expert_out = jnp.einsum('eti,edi->etd', h, W2)
            y = jnp.einsum('etd,te->td', expert_out, combine)
            z = jax.nn.silu(xt @ Ws1.T) * (xt @ Ws3.T) @ Ws2.T
            return (y + z).reshape(B, S, D)
        key = jax.random.key(seed)
        ks = jax.random.split(key, 8)
        s = 0.02
        x = jax.random.normal(ks[0], (1, 512, DIM), dtype=jnp.float32)
        Wg = jax.random.normal(ks[1], (E, DIM), dtype=jnp.float32) * s
        W1 = jax.random.normal(ks[2], (E, INTER, DIM), dtype=jnp.float32) * s
        W3 = jax.random.normal(ks[3], (E, INTER, DIM), dtype=jnp.float32) * s
        W2 = jax.random.normal(ks[4], (E, DIM, INTER), dtype=jnp.float32) * s
        Ws1 = jax.random.normal(ks[5], (SHARED_INTER, DIM), dtype=jnp.float32) * s
        Ws3 = jax.random.normal(ks[6], (SHARED_INTER, DIM), dtype=jnp.float32) * s
        Ws2 = jax.random.normal(ks[7], (DIM, SHARED_INTER), dtype=jnp.float32) * s
        return {'x': x, 'Wg': Wg, 'W1': W1, 'W3': W3, 'W2': W2, 'Ws1': Ws1, 'Ws3': Ws3, 'Ws2': Ws2}
    _L0_ffn_all = _L0_ffn_setup()
    _L0_ffn_in = {k: v for k, v in _L0_ffn_all.items() if k in ('Wg', 'W1', 'W3', 'W2', 'Ws1', 'Ws3', 'Ws2')}
    del _L0_ffn_all
    return {'x': x, 'ctx_2048': ctx_2048, 'L0_xattn_Wh': _L0_xattn_in['Wh'], 'L0_xattn_wg_w': _L0_xattn_in['wg_w'], 'L0_xattn_wo_w': _L0_xattn_in['wo_w'], 'L0_xattn_gn_gamma': _L0_xattn_in['gn_gamma'], 'L0_xattn_gn_beta': _L0_xattn_in['gn_beta'], 'L0_ffn_Wg': _L0_ffn_in['Wg'], 'L0_ffn_W1': _L0_ffn_in['W1'], 'L0_ffn_W3': _L0_ffn_in['W3'], 'L0_ffn_W2': _L0_ffn_in['W2'], 'L0_ffn_Ws1': _L0_ffn_in['Ws1'], 'L0_ffn_Ws3': _L0_ffn_in['Ws3'], 'L0_ffn_Ws2': _L0_ffn_in['Ws2']}

def reference(x, ctx_2048, L0_xattn_Wh, L0_xattn_wg_w, L0_xattn_wo_w, L0_xattn_gn_gamma, L0_xattn_gn_beta, L0_ffn_Wg, L0_ffn_W1, L0_ffn_W3, L0_ffn_W2, L0_ffn_Ws1, L0_ffn_Ws3, L0_ffn_Ws2):
    import jax
    import jax.numpy as jnp

    def _L0_xattn_ref(x, k, v, Wh, wg_w, wo_w, gn_gamma, gn_beta):
        import jax, jax.numpy as jnp
        import numpy as np
        B, S, DIM, HD = (4, 256, 512, 128)
        H = DIM // HD
        GN_EPS = 0.001

        def _decay_masks(n_heads, seq_len):
            gam = 1.0 - 2.0 ** (-5.0 - jnp.arange(n_heads, dtype=jnp.float32))
            idx = jnp.arange(seq_len, dtype=jnp.float32)
            expo = idx[None, :] - idx[:, None]
            D = jnp.where(expo[None, :, :] <= 0, gam[:, None, None] ** expo[None, :, :], 0.0)
            return D / jnp.sqrt(D.sum(axis=-1))[:, None, :]
        b, s, dim = x.shape
        h, hd, _ = Wh.shape
        xh = x.reshape(b, s, h, hd)
        kh = k.reshape(b, s, h, hd)
        vh = v.reshape(b, s, h, hd)
        Q = jnp.einsum('bshd,hde->bshe', xh, Wh)
        K = jnp.einsum('bshd,hde->bshe', kh, Wh)
        V = jnp.einsum('bshd,hde->bshe', vh, Wh)
        scores = jnp.einsum('bshe,bthe->bhst', Q, K) / jnp.sqrt(jnp.float32(hd))
        Dn = _decay_masks(h, s)
        masked = scores * Dn[None, :, :, :]
        A = jnp.maximum(jnp.abs(masked.sum(axis=0)), 1.0)
        O = jnp.einsum('hst,bthe->bshe', A, V).reshape(b, s, dim)
        mu = O.mean(axis=-1, keepdims=True)
        var = O.var(axis=-1, keepdims=True)
        Y = (O - mu) / jnp.sqrt(var + GN_EPS) * gn_gamma + gn_beta
        W = jax.nn.relu(x @ wg_w)
        return W * Y @ wo_w

    def _L0_ffn_ref(x, Wg, W1, W3, W2, Ws1, Ws3, Ws2):
        import jax, jax.numpy as jnp
        import numpy as np
        DIM = 512
        INTER = 352
        E = 16
        TOPK = 4
        G = 4
        TOPK_G = 2
        N_SHARED = 2
        SHARED_INTER = N_SHARED * INTER
        ROUTE_SCALE = 1.0

        def _moe_forward(x, Wg, W1, W3, W2, Ws1, Ws3, Ws2):
            B, S, D = x.shape
            xt = x.reshape(-1, D)
            T = xt.shape[0]
            scores = jax.nn.softmax(xt @ Wg.T, axis=-1)
            sg = scores.reshape(T, G, E // G)
            group_scores = sg.max(axis=-1)
            gidx = jax.lax.top_k(group_scores, TOPK_G)[1]
            gmask = jax.nn.one_hot(gidx, G, dtype=jnp.float32).sum(axis=1) > 0
            masked = jnp.where(gmask[:, :, None], sg, -jnp.inf).reshape(T, E)
            topi = jax.lax.top_k(masked, TOPK)[1]
            weights = jnp.take_along_axis(scores, topi, axis=1) * ROUTE_SCALE
            combine = jnp.zeros((T, E), xt.dtype).at[jnp.arange(T)[:, None], topi].add(weights)
            h = jax.nn.silu(jnp.einsum('td,eid->eti', xt, W1)) * jnp.einsum('td,eid->eti', xt, W3)
            expert_out = jnp.einsum('eti,edi->etd', h, W2)
            y = jnp.einsum('etd,te->td', expert_out, combine)
            z = jax.nn.silu(xt @ Ws1.T) * (xt @ Ws3.T) @ Ws2.T
            return (y + z).reshape(B, S, D)
        return _moe_forward(x, Wg, W1, W3, W2, Ws1, Ws3, Ws2)
    x = x + _L0_xattn_ref(_layernorm(x, axis=-1), ctx_2048, ctx_2048, L0_xattn_Wh, L0_xattn_wg_w, L0_xattn_wo_w, L0_xattn_gn_gamma, L0_xattn_gn_beta)
    x = x + _L0_ffn_ref(_layernorm(x, axis=-1), L0_ffn_Wg, L0_ffn_W1, L0_ffn_W3, L0_ffn_W2, L0_ffn_Ws1, L0_ffn_Ws3, L0_ffn_Ws2)
    return x

_drawn_inputs = setup_inputs


def setup_inputs(seed=0):
    import zlib

    import numpy as np

    out = dict(_drawn_inputs(seed))
    spreads = {'L0_xattn_gn_gamma': (1.0, 0.2), 'L0_xattn_gn_beta': (0.0, 0.1)}
    factors = {'L0_ffn_Wg': 8.0,
     'L0_ffn_W1': 8.0,
     'L0_ffn_W3': 7.864,
     'L0_ffn_W2': 7.886,
     'L0_ffn_Ws1': 8.0,
     'L0_ffn_Ws3': 8.0,
     'L0_ffn_Ws2': 8.0}
    for name, (base, spread) in spreads.items():
        noise = np.random.default_rng([zlib.crc32(name.encode()), seed]).standard_normal(out[name].shape)
        drawn = base * np.exp(spread * noise) if base else spread * noise
        out[name] = jnp.asarray(drawn.astype(out[name].dtype))
    for name, factor in factors.items():
        out[name] = (out[name] * factor).astype(out[name].dtype)
    return out
```

```python
from contextlib import ExitStack

import concourse.bass as bass
from concourse import mybir

ALU = mybir.AluOpType
ACT = mybir.ActivationFunctionType
F32 = mybir.dt.float32
F32R = mybir.dt.float32r
BF16 = mybir.dt.bfloat16
I32 = mybir.dt.int32
U32 = mybir.dt.uint32
AX = mybir.AxisListType.X

P = 128
B, S, D = 4, 512, 512
H, HD = 4, 128
KT = D // P
ST = S // P
TOK = B * S
NT = TOK // P
E, G, TOPG, TOPK = 16, 4, 2, 4
EG = E // G
INTER = 352
IC = 3
N_SHARED = 2
NW = E + N_SHARED
W13 = KT * 2 * INTER
WCOL = W13 + IC * D
NR = TOK * TOPK // P + E
LN_EPS, GN_EPS = 1e-5, 1e-3
SENTINEL = -9.0

C_ID, C_UP, C_ONE = 0, 128, 256
C_IOTA, C_CAP, C_LT, C_LG, C_TILE, C_KDEC = 384, 400, 416, 672, 688, 768
C_EPS = 784
C_ALL = 786
HC_W, HC_WT = TOK, TOK + HD
HCOL = TOK + 2 * HD
AT_OFF = [0, 512, 896, 1152]
AT_COL = 1280


def pipeline(eng, tiles, parts, ramp=2):
    most = max(a for a, _ in parts)
    least = min(a for a, _ in parts)
    lo = min(max(0, ramp - least), tiles)
    hi = tiles - max(0, most)
    hi -= (hi - lo) % 2

    def peeled(s):
        for ahead, fn in parts:
            t = s + ahead
            if 0 <= t < tiles:
                fn(t, t % 2, t // 2)

    for s in range(-max(0, most), lo):
        peeled(s)
    hi = max(hi, lo)
    with eng.Fori(0, (hi - lo) // 2) as j:
        for u in range(2):
            for ahead, fn in parts:
                t = lo + u + ahead
                fn(2 * j + t, t % 2, j + t // 2)
    for s in range(hi, tiles - min(0, least)):
        peeled(s)


def xattn_moe(nc, x, heads, wg, wo, gn, wr, wexp, tables, qdecay, out):
    outer = ExitStack()
    with outer:
        def psum(name, shape, dt):
            return outer.enter_context(nc.psum_tensor(name, shape, dt))

        def sem(name):
            return outer.enter_context(nc.semaphore(name))

        def keep(name, shape, dt):
            return outer.enter_context(nc.sbuf_tensor(name, shape, dt))

        const = keep("const", [P, C_ALL], F32)
        cbf = keep("cbf", [P, 2, P], BF16)
        res = keep("res", [P, NT * D], F32)
        xnT = res[:, :].rearrange("p (h n) -> p h n", h=H)
        x1 = res[:, :].rearrange("p (t n) -> p t n", t=NT)
        raw = keep("raw", [P, 2, WCOL], F32)
        logits = keep("logits", [P, NT, E], F32)
        ident = const[:, C_ID:C_ID + P]
        ones = const[:, C_ONE:C_ONE + P]

        with ExitStack() as early:
            def sb1(name, shape, dt):
                return early.enter_context(nc.sbuf_tensor(name, shape, dt))
            head_in = sb1("head_in", [P, 2, HCOL], F32)
            v_sb = sb1("v_sb", [P, ST, B * HD], F32)
            q_sb = sb1("q_sb", [P, B, S], F32)
            at_sb = sb1("at_sb", [P, AT_COL], F32)
            g_sb = sb1("g_sb", [P, HD], F32)
            wg_sb = sb1("wg_sb", [P, KT, D], F32)
            qdec = sb1("qdec", [P, H, S], F32)
            gate_out = sb1("gate_out", [P, 2, D], F32)
        whi = keep("whi", [P, 2, WCOL], F32R)
        wlo = keep("wlo", [P, 2, WCOL], F32R)

        with ExitStack() as mid:
            def sb2(name, shape, dt):
                return mid.enter_context(nc.sbuf_tensor(name, shape, dt))
            o_sb = sb2("o_sb", [P, NT, D], F32)
            xin = sb2("xin", [P, 2, D], F32)
            gin = sb2("gin", [P, 2, D], F32)
            xr = sb2("xr", [P, 2, D], F32)
            xT = sb2("xT", [P, 2, KT, P], F32)
            xT2 = sb2("xT2", [P, 2, KT, P], F32)
            wo_sb = sb2("wo_sb", [P, KT, D], F32)
            gn_sb = sb2("gn_sb", [P, 2, D], F32)
            wr_sb = sb2("wr_sb", [P, KT, E], F32)
            zero = sb2("zero", [P, D], F32)
            st1 = sb2("st1", [P, 2, 6], F32)
            mv1 = sb2("mv1", [P, 2, 2], F32)
            sd1 = sb2("sd1", [P, 2, 2], F32)
            st3 = sb2("st3", [P, NT, H, 6], F32)
            mv3 = sb2("mv3", [P, NT, 2], F32)
            sd3 = sb2("sd3", [P, 2, NT], F32)

        def sb3(name, shape, dt):
            return keep(name, shape, dt)
        xg = sb3("xg", [P, 2, D], F32)
        xhi = sb3("xhi", [P, 2, KT * P], F32R)
        xlo = sb3("xlo", [P, 2, KT * P], F32R)
        sg = sb3("sg", [P, INTER], F32)
        hx = sb3("hx", [P, IC * P], F32)
        hhi = sb3("hhi", [P, IC * P], F32R)
        hlo = sb3("hlo", [P, IC * P], F32R)
        ysb = sb3("ysb", [P, 2, D], F32)
        scat = sb3("scat", [P, 2, D], F32)
        gath = sb3("gath", [P, 2, TOPK, D], F32)
        osb = sb3("osb", [P, 2, D], F32)
        rmax = sb3("rmax", [P, 2, NT], F32)
        score = sb3("score", [P, NT, E], F32)
        gsc = sb3("gsc", [P, NT, G], F32)
        gcmp = sb3("gcmp", [P, 2, NT, G * G], F32)
        gkeep = sb3("gkeep", [P, NT, G], F32)
        masked = sb3("masked", [P, NT, E], F32)
        top8 = sb3("top8", [P, NT, 8], F32)
        top8i = sb3("top8i", [P, NT, 8], U32)
        top8f = sb3("top8f", [P, NT, 8], F32)
        onehot = sb3("onehot", [P, NT, TOPK * E], F32)
        sel = sb3("sel", [P, NT * E], BF16)
        self32 = sb3("self32", [P, NT, E], F32)
        tcmp = sb3("tcmp", [P, E * E], F32)
        ntile = sb3("ntile", [P, 2, E], F32)
        slot = sb3("slot", [P, NT * E], F32)
        pick = gath[:, 0, :, :].rearrange("p k n -> p (k n)")[:, 0:NT * TOPK * E].rearrange("p (t n) -> p t n", t=NT)
        slotf = sb3("slotf", [P, NT * TOPK], F32)
        sloti = sb3("sloti", [P, NT * TOPK], I32)
        slotc = sb3("slotc", [P, 2, TOPK], I32)
        ecmp = gath[0:1, 1, :, :].rearrange("p k n -> p (k n)")[:, 0:NR * E].rearrange("p (t e) -> p t e", t=NR)
        tabf = sb3("tabf", [1, NR + E], F32)
        order = sb3("order", [1, NR + E], I32)
        side = sb3("side", [1, NR], I32)

        ps = psum("ps", [P, 8, 512], F32)

        gate_d = nc.dram_tensor("gate_d", [TOK, D], F32, kind="Internal").ap()
        xn_d = nc.dram_tensor("xn_d", [TOK, D], F32, kind="Internal").ap()
        xslot_d = nc.dram_tensor("xslot_d", [NR * P, D], F32, kind="Internal").ap()
        yslot_d = nc.dram_tensor("yslot_d", [NR * P, D], F32, kind="Internal").ap()

        c_loaded, w1_loaded, w3_loaded = sem("c_loaded"), sem("w1_loaded"), sem("w3_loaded")
        x_loaded = [sem(f"x_loaded{p}") for p in range(2)]
        cbf_ready, zero_ready, zeroed = sem("cbf_ready"), sem("zero_ready"), sem("zeroed")
        s1_stats, s1_aggr, s1_std, s1_rstd, s1_xn = (sem(f"s1_{n}") for n in ("stats", "aggr", "std", "rstd", "xn"))
        s1_tr = sem("s1_tr")
        s1_xT, s1_xnT = sem("s1_xT"), sem("s1_xnT")
        s1_mm = sem("s1_mm")
        s1_gate = sem("s1_gate")
        gate_stored = [sem(f"gate_stored{p}") for p in range(2)]
        head_loaded = [sem(f"head_loaded{p}") for p in range(2)]
        g_mm, g_ready, v_mm, v_ready, q_mm, q_ready = (sem(n) for n in ("g_mm", "g_ready", "v_mm", "v_ready", "q_mm", "q_ready"))
        s_mm, s_abs, at_max, at_ready, o_mm, o_ready = (sem(n) for n in ("s_mm", "s_abs", "at_max", "at_ready", "o_mm", "o_ready"))
        o_stats, o_aggr, o_std, o_rstd = (sem(n) for n in ("o_stats", "o_aggr", "o_std", "o_rstd"))
        gate_loaded = [sem(f"gate_loaded{p}") for p in range(2)]
        x3_loaded = [sem(f"x3_loaded{p}") for p in range(2)]
        o_normed, o_gamma, o_beta, gated = (sem(n) for n in ("o_normed", "o_gamma", "o_beta", "gated"))
        a_tr, a_xT, a_mm = (sem(n) for n in ("a_tr", "a_xT", "a_mm"))
        x1_ready, l_stats, l_aggr, l_std, l_rstd, xn_ready = (sem(n) for n in ("x1_ready", "l_stats", "l_aggr", "l_std", "l_rstd", "xn_ready"))
        b_tr, b_xT, r_mm, r_ready = (sem(n) for n in ("b_tr", "b_xT", "r_mm", "r_ready"))
        xn_stored = [sem(f"xn_stored{p}") for p in range(2)]
        rt, rt_exp, rt_sel, rt_mm, rt_done = (sem(n) for n in ("rt", "rt_exp", "rt_sel", "rt_mm", "rt_done"))
        raw_loaded = [sem(f"raw_loaded{p}") for p in range(2)]
        w_hi, w_ready = sem("w_hi"), sem("w_ready")
        xg_loaded = [sem(f"xg_loaded{p}") for p in range(2)]
        x_tr = sem("x_tr")
        x_hi, x_lo = sem("x_hi"), sem("x_lo")
        mm1 = sem("mm1")
        silu, h_ready, h_tr, h_hi, h_lo, h_pad = (sem(n) for n in ("silu", "h_ready", "h_tr", "h_hi", "h_lo", "h_pad"))
        mm2 = sem("mm2")
        y_out = sem("y_out")
        y_stored = [sem(f"y_stored{p}") for p in range(2)]
        scat_loaded = [sem(f"scat_loaded{p}") for p in range(2)]
        scattered = [sem(f"scattered{p}") for p in range(2)]
        slotc_ready = sem("slotc_ready")
        gathered = [sem(f"gathered{p}") for p in range(2)]
        comb = sem("comb")
        out_stored = [sem(f"out_stored{p}") for p in range(2)]

        block = outer.enter_context(nc.Block())

        def hold(eng, sem, value):
            if type(value) is not int:
                value = eng.snap(eng.to_reg(value))
            eng.wait_ge(c_loaded, 16)
            eng.wait_ge(sem, value)

        def rows(dram, t):
            return dram[bass.ds(t * P, P), :]

        @block.sync
        def _(sp):
            sp.dma_start(const[:, :], tables).then_inc(c_loaded, 16)
            sp.dma_start(wg_sb[:, :, :], wg.rearrange("(k p) n -> p k n", p=P)).then_inc(w1_loaded, 16)

            def load_x(t, p, half):
                sp.wait_ge(s1_tr, t + 1)
                sp.dma_start(xin[:, p, :], rows(x, t)).then_inc(x_loaded[p], 16)

            def store_gate(t, p, half):
                sp.wait_ge(s1_gate, 2 + t + 1)
                sp.dma_start(rows(gate_d, t), gate_out[:, p, :]).then_inc(gate_stored[p], 16)

            def load_head(h, p, half):
                if h >= 2:
                    sp.wait_ge(s_mm, 4 * (h - 1))
                sp.dma_start(head_in[:, p, :], heads[h, :, :]).then_inc(head_loaded[p], 16)

            pipeline(sp, NT, [(1, load_x), (-1, store_gate)])
            load_head(0, 0, 0)
            load_head(1, 1, 0)
            sp.dma_start(qdec[:, :, :], qdecay[None, :, :].to_broadcast([P, H, S])).then_inc(w1_loaded, 16)
            sp.dma_start(wo_sb[:, :, :], wo.rearrange("(k p) n -> p k n", p=P)).then_inc(w3_loaded, 16)
            sp.dma_start(gn_sb[:, :, :], gn[None, :, :].to_broadcast([P, 2, D])).then_inc(w3_loaded, 16)
            sp.dma_start(wr_sb[:, :, :], wr.rearrange("(k p) n -> p k n", p=P)).then_inc(w3_loaded, 16)
            sp.wait_ge(zero_ready, 1)
            for c in range(NR // 8):
                sp.dma_start(xslot_d[c * 8 * P:(c + 1) * 8 * P, :].rearrange("(p r) n -> p r n", p=P),
                             zero[:, None, :].to_broadcast([P, 8, D])).then_inc(zeroed, 16)
            load_head(2, 0, 1)
            load_head(3, 1, 1)

            for p in range(2):
                sp.wait_ge(gate_stored[p], 16 * (NT // 2))
            sp.wait_ge(s1_tr, 2 + NT)

            def load_3(t, p, half):
                if type(t) is not int or t >= 2:
                    sp.wait_ge(a_tr, t - 1)
                    sp.wait_ge(x1_ready, t - 1)
                sp.dma_start(gin[:, p, :], rows(gate_d, t)).then_inc(gate_loaded[p], 16)
                sp.dma_start(xin[:, p, :], rows(x, t)).then_inc(x3_loaded[p], 16)

            def store_xn(t, p, half):
                sp.wait_ge(xn_ready, t + 1)
                sp.dma_start(rows(xn_d, t), xr[:, p, :]).then_inc(xn_stored[p], 16)

            pipeline(sp, NT, [(2, load_3), (0, store_xn)])

            for p in range(2):
                sp.wait_ge(xn_stored[p], 16 * (NT // 2))
            sp.wait_ge(r_ready, NT)

            def load_tile(base, src):
                def fn(t, p, half):
                    sp.wait_ge(x_tr, base + t + 1)
                    sp.dma_start(xg[:, p, :], rows(src, t)).then_inc(xg_loaded[p], 16)
                return fn

            def store_y(t, p, half):
                sp.wait_ge(y_out, 2 + NT + t + 1)
                sp.dma_start(rows(yslot_d, t), ysb[:, p, :]).then_inc(y_stored[p], 16)

            def store_out(t, p, half):
                sp.wait_ge(comb, (1 + TOPK) * (t + 1))
                sp.dma_start(rows(out, t), osb[:, p, :]).then_inc(out_stored[p], 16)

            pipeline(sp, NT, [(1, load_tile(0, xn_d))])
            for p in range(2):
                sp.wait_ge(scattered[p], 16 * TOPK * (NT // 2))
            pipeline(sp, NR, [(1, load_tile(NT, xslot_d)), (-1, store_y)])
            pipeline(sp, NT, [(1, load_tile(NT + NR, xn_d)), (-1, store_out)])
            for p in range(2):
                sp.wait_ge(out_stored[p], 16 * (NT // 2))

        @block.gpsimd
        def _(pool):
            pool.memset(zero[:, :], 0.0).then_inc(zero_ready, 1)
            pool.wait_ge(c_loaded, 16)
            pool.tensor_copy(cbf[:, :, :], const[:, C_UP:C_UP + 2 * P].rearrange("p (a n) -> p a n", a=2)).then_inc(cbf_ready, 1)

            pool.wait_ge(s1_tr, 2 + NT)
            for p in range(2):
                pool.dma_start(raw[:, p, :], wexp[p, :, :]).then_inc(raw_loaded[p], 16)

            def diagonals(h, p, half):
                for j in range(ST):
                    pool.wait_ge(at_max, ST * h + j + 1)
                    blk = at_sb[:, AT_OFF[j]:AT_OFF[j] + P]
                    pool.affine_select(out=blk, in_=blk, compare_op=ALU.is_ge, fill=1.0, base=0,
                                       pattern=[[1, P]], channel_multiplier=-1).then_inc(at_ready, 1)

            for h in range(H):
                diagonals(h, h % 2, h // 2)

            def split(o, p, half, free):
                hold(pool, raw_loaded[p], 16 * (half + 1))
                free(o)
                pool.tensor_copy(whi[:, p, :], raw[:, p, :]).then_inc(w_hi, 1)
                hold(pool, w_hi, o + 1)
                pool.tensor_tensor(wlo[:, p, :], raw[:, p, :], whi[:, p, :].bitcast(F32), ALU.subtract).then_inc(w_ready, 1)

            def next_raw(o, p):
                hold(pool, w_ready, o + 1)
                pool.dma_start(raw[:, p, :], wexp[bass.ds(o + 2, 1), :, :].rearrange("a p n -> p (a n)")).then_inc(raw_loaded[p], 16)

            def affine(t, p, half):
                hold(pool, o_normed, t + 1)
                pool.tensor_tensor(o_sb[:, bass.ds(t, 1), :], o_sb[:, bass.ds(t, 1), :], gn_sb[:, 0:1, :], ALU.mult).then_inc(o_gamma, 1)
                hold(pool, o_gamma, t + 1)
                pool.tensor_tensor(o_sb[:, bass.ds(t, 1), :], o_sb[:, bass.ds(t, 1), :], gn_sb[:, 1:2, :], ALU.add).then_inc(o_beta, 1)

            pool.wait_ge(w3_loaded, 48)
            pipeline(pool, NT, [(0, affine)], ramp=0)

            def stage2_over(o):
                pool.wait_ge(o_mm, ST * H)
                for p in range(2):
                    pool.wait_ge(gate_stored[p], 16 * (NT // 2))

            for o in range(2):
                split(o, o, 0, stage2_over)
                next_raw(o, o)

            pool.wait_ge(rt_done, 1)
            pool.wait_ge(zeroed, 16 * (NR // 8))

            def load_scat(t, p, half):
                if type(t) is not int or t >= 2:
                    hold(pool, scattered[p], 16 * TOPK * half)
                pool.dma_start(scat[:, p, :], rows(xn_d, t)).then_inc(scat_loaded[p], 16)
                pool.tensor_copy(slotc[:, p, :], sloti[:, bass.ds(t * TOPK, TOPK)]).then_inc(slotc_ready, 1)

            def scatter(t, p, half):
                hold(pool, scat_loaded[p], 16 * (half + 1))
                hold(pool, slotc_ready, t + 1)
                for k in range(TOPK):
                    pool.indirect_dma_start(
                        out=xslot_d, out_offset=bass.IndirectOffsetOnAxis(ap=slotc[:, p, k:k + 1], axis=0),
                        in_=scat[:, p, :], in_offset=None).then_inc(scattered[p], 16)

            pipeline(pool, NT, [(1, load_scat), (0, scatter)])

            def tiles_through(o):
                before = pool.value_load(order[0:1, bass.ds(o + NR - 2, 1)], min_val=NT, max_val=NT + NR)
                hold(pool, mm2, before)

            def set_and_next(o, p, half):
                split(o + 2, p, half + 1, lambda o: tiles_through(o))
                next_raw(o + 2, p)

            pipeline(pool, NW - 4, [(0, set_and_next)], ramp=0)
            for o in range(NW - 2, NW):
                split(o, o % 2, o // 2, tiles_through)

            for p in range(2):
                pool.wait_ge(y_stored[p], 16 * (NR // 2))

            def gather(t, p, half):
                if type(t) is not int or t >= 2:
                    hold(pool, comb, (1 + TOPK) * (t - 1))
                pool.tensor_copy(slotc[:, p, :], sloti[:, bass.ds(t * TOPK, TOPK)]).then_inc(slotc_ready, 1)
                hold(pool, slotc_ready, NT + t + 1)
                for k in range(TOPK):
                    pool.indirect_dma_start(
                        out=gath[:, p, k, :], out_offset=None, in_=yslot_d,
                        in_offset=bass.IndirectOffsetOnAxis(ap=slotc[:, p, k:k + 1], axis=0)).then_inc(gathered[p], 16)

            pipeline(pool, NT, [(2, gather)])

        @block.scalar
        def _(act):
            act.sem_inc(s1_gate, 2)
            act.sem_inc(y_out, 2)
            act.wait_ge(c_loaded, 16)

            def std_1(t, p, half):
                act.wait_ge(s1_aggr, t + 1)
                act.activation(sd1[:, p, 0:1], mv1[:, p, 1:2], ACT.Sqrt, bias=const[:, C_EPS:C_EPS + 1]).then_inc(s1_std, 1)

            def evac_1(t, p, half):
                act.wait_ge(s1_tr, 2 + t + 1)
                act.wait_ge(s1_mm, t + 1)
                act.wait_ge(s1_xnT, t)
                act.activation(xT[:, p, :, :], ps[:, p, :], ACT.Copy).then_inc(s1_xT, 1)

            def relu_1(t, p, half):
                act.wait_ge(s1_mm, 2 + t + 1)
                if type(t) is not int or t >= 2:
                    act.wait_ge(gate_stored[p], 16 * half)
                act.activation(gate_out[:, p, :], ps[:, 2 + p, :], ACT.Relu).then_inc(s1_gate, 1)

            pipeline(act, NT, [(1, std_1), (0, evac_1), (-1, relu_1)])

            def head(h, p, half):
                act.wait_ge(o_mm, ST * h)
                for tt in range(ST):
                    act.wait_ge(v_mm, ST * h + tt + 1)
                    act.activation(v_sb[:, tt, :], ps[:, (1 + tt) % 2, :], ACT.Copy).then_inc(v_ready, 1)
                for j in range(ST):
                    act.wait_ge(s_mm, ST * h + j + 1)
                    n = S - P * j
                    act.activation(at_sb[:, AT_OFF[j]:AT_OFF[j] + n], ps[:, 4 + j % 2, 0:n], ACT.Abs,
                                   scale=const[:, bass.ds(C_KDEC + h * ST + j, 1)]).then_inc(s_abs, 1)
                for i in range(ST):
                    act.wait_ge(o_mm, ST * h + i + 1)
                    act.activation(o_sb[:, :, :].rearrange("p (b i) n -> p b i n", i=ST)[:, :, i, bass.ds(h * HD, HD)],
                                   ps[:, 6 + i % 2, :].rearrange("p (b n) -> p b n", b=B), ACT.Copy).then_inc(o_ready, 1)

            for h in range(H):
                head(h, h % 2, h // 2)

            act.wait_ge(o_aggr, NT)
            act.activation(sd3[:, 0, :], mv3[:, :, 1], ACT.Sqrt, bias=const[:, C_EPS + 1:C_EPS + 2]).then_inc(o_std, 1)

            def evac_a(t, p, half):
                act.wait_ge(a_tr, t + 1)
                if type(t) is not int or t >= 2:
                    act.wait_ge(a_mm, t - 1)
                act.activation(xT[:, p, :, :], ps[:, p, :], ACT.Copy).then_inc(a_xT, 1)

            def evac_b(t, p, half):
                act.wait_ge(b_tr, t + 1)
                if type(t) is not int or t >= 2:
                    act.wait_ge(r_mm, t - 1)
                act.activation(xT2[:, p, :, :], ps[:, 4 + p, :], ACT.Copy).then_inc(b_xT, 1)

            def std_3(t, p, half):
                act.wait_ge(l_aggr, t + 1)
                act.activation(sd1[:, p, 0:1], mv1[:, p, 1:2], ACT.Sqrt, bias=const[:, C_EPS:C_EPS + 1]).then_inc(l_std, 1)

            pipeline(act, NT, [(1, evac_a), (-1, evac_b), (0, std_3)])

            act.wait_ge(rt, 2)
            act.activation(score[:, :, :], score[:, :, :], ACT.Exp).then_inc(rt_exp, 1)

            def silu_g(base):
                def fn(t, p, half):
                    act.wait_ge(mm1, 2 + base + t + 1)
                    act.wait_ge(h_ready, base + t)
                    act.activation(sg[:, :], ps[:, 2, 0:INTER], ACT.Silu).then_inc(silu, 1)
                return fn

            def x_high(base):
                def fn(t, p, half):
                    act.wait_ge(x_tr, 2 + base + t + 1)
                    act.wait_ge(mm1, base + t + 1)
                    act.activation(xhi[:, p, :], ps[:, p, :], ACT.Copy).then_inc(x_hi, 1)
                return fn

            def h_high(base):
                def fn(t, p, half):
                    act.wait_ge(h_tr, base + t + 1)
                    act.wait_ge(mm2, base + t)
                    act.activation(hhi[:, :], ps[:, 4, 0:IC * P], ACT.Copy).then_inc(h_hi, 1)
                return fn

            def y_evac(t, p, half):
                act.wait_ge(mm2, NT + t + 1)
                if type(t) is not int or t >= 2:
                    act.wait_ge(y_stored[p], 16 * half)
                act.activation(ysb[:, p, :], ps[:, 5 + p, :], ACT.Copy).then_inc(y_out, 1)

            pipeline(act, NT, [(0, silu_g(0)), (1, x_high(0)), (0, h_high(0))])
            pipeline(act, NR, [(0, silu_g(NT)), (1, x_high(NT)), (-1, y_evac), (0, h_high(NT))])
            pipeline(act, NT, [(0, silu_g(NT + NR)), (1, x_high(NT + NR)), (0, h_high(NT + NR))])

        @block.tensor
        def _(pe):
            pe.sem_inc(s1_tr, 2)
            pe.sem_inc(s1_mm, 2)
            pe.sem_inc(x_tr, 2)
            pe.sem_inc(mm1, 2)
            pe.wait_ge(c_loaded, 16)

            def transposes(dst, src, n, done):
                for k in range(n):
                    mm = pe.transpose(dst[:, k * P:(k + 1) * P], src[:, k * P:(k + 1) * P], ident)
                mm.then_inc(done, 1)

            def tr_1(t, p, half):
                pe.wait_ge(s1_xn, t + 1)
                if type(t) is not int or t >= 2:
                    pe.wait_ge(s1_xT, t - 1)
                transposes(ps[:, p, :], xin[:, p, :], KT, s1_tr)

            def gate_1(t, p, half):
                pe.wait_ge(s1_xT, t + 1)
                pe.wait_ge(s1_gate, t + 1)
                for k in range(KT):
                    mm = pe.matmul(ps[:, 2 + p, :], xT[:, p, k, :], wg_sb[:, k, :], start=(k == 0), stop=(k == KT - 1))
                mm.then_inc(s1_mm, 1)

            pe.wait_ge(w1_loaded, 16)
            pipeline(pe, NT, [(1, tr_1), (0, gate_1)])

            pe.wait_ge(s1_gate, 2 + NT)
            pe.wait_ge(s1_xnT, NT)

            def head(h, p, half):
                ctxT = head_in[:, p, 0:TOK]
                w = head_in[:, p, HC_W:HC_W + HD]
                wT = head_in[:, p, HC_WT:HC_WT + HD]
                pe.wait_ge(head_loaded[p], 16 * (half + 1))
                pe.wait_ge(v_ready, ST * h)
                pe.matmul(ps[:, 0, 0:HD], wT, wT, start=True, stop=True).then_inc(g_mm, 1)
                for tt in range(ST):
                    if tt == 1:
                        pe.wait_ge(g_ready, h + 1)
                    if tt >= 2:
                        pe.wait_ge(v_ready, ST * h + tt - 1)
                    for b in range(B):
                        mm = pe.matmul(ps[:, (1 + tt) % 2, b * HD:(b + 1) * HD], ctxT[:, b * S + tt * P:b * S + (tt + 1) * P], w,
                                       start=True, stop=True)
                    mm.then_inc(v_mm, 1)
                for b in range(B):
                    pe.wait_ge(q_ready, B * h + max(b - 1, 0))
                    pe.matmul(ps[:, 2 + b % 2, :], g_sb[:, :], xnT[:, bass.ds(h, 1), b * S:(b + 1) * S],
                              start=True, stop=True).then_inc(q_mm, 1)
                pe.wait_ge(q_ready, B * h + B)
                for j in range(ST):
                    pe.wait_ge(s_abs, ST * h + max(j - 1, 0))
                    for b in range(B):
                        mm = pe.matmul(ps[:, 4 + j % 2, 0:S - P * j], ctxT[:, b * S + j * P:b * S + (j + 1) * P],
                                       q_sb[:, b, P * j:S], start=(b == 0), stop=(b == B - 1))
                    mm.then_inc(s_mm, 1)
                pe.wait_ge(v_ready, ST * h + ST)
                for i in range(ST):
                    pe.wait_ge(at_ready, ST * h + i + 1)
                    pe.wait_ge(o_ready, ST * h + max(i - 1, 0))
                    for j in range(ST):
                        a = at_sb[:, AT_OFF[j] + (i - j) * P:AT_OFF[j] + (i - j + 1) * P] if j <= i else ones
                        mm = pe.matmul(ps[:, 6 + i % 2, :], a, v_sb[:, j, :], start=(j == 0), stop=(j == ST - 1))
                    mm.then_inc(o_mm, 1)

            for h in range(H):
                head(h, h % 2, h // 2)

            pe.wait_ge(o_ready, ST * H)
            pe.wait_ge(w3_loaded, 48)

            def tr_a(t, p, half):
                pe.wait_ge(gated, t + 1)
                if type(t) is not int or t >= 2:
                    pe.wait_ge(a_xT, t - 1)
                transposes(ps[:, p, :], gin[:, p, :], KT, a_tr)

            def proj(t, p, half):
                pe.wait_ge(a_xT, t + 1)
                if type(t) is not int or t >= 2:
                    pe.wait_ge(x1_ready, t - 1)
                for k in range(KT):
                    mm = pe.matmul(ps[:, 2 + p, :], xT[:, p, k, :], wo_sb[:, k, :], start=(k == 0), stop=(k == KT - 1))
                mm.then_inc(a_mm, 1)

            def tr_b(t, p, half):
                pe.wait_ge(xn_ready, t + 1)
                if type(t) is not int or t >= 2:
                    pe.wait_ge(b_xT, t - 1)
                transposes(ps[:, 4 + p, :], xr[:, p, :], KT, b_tr)

            def router(t, p, half):
                pe.wait_ge(b_xT, t + 1)
                if type(t) is not int or t >= 2:
                    pe.wait_ge(r_ready, t - 1)
                for k in range(KT):
                    mm = pe.matmul(ps[:, 6 + p, 0:E], xT2[:, p, k, :], wr_sb[:, k, :], start=(k == 0), stop=(k == KT - 1))
                mm.then_inc(r_mm, 1)

            pipeline(pe, NT, [(1, tr_a), (0, proj), (-1, tr_b), (-2, router)])

            pe.wait_ge(rt_sel, 1)
            pe.wait_ge(cbf_ready, 1)
            pe.wait_ge(r_ready, NT)
            pe.matmul(ps[:, 7, 0:NT * E], cbf[:, 0, :], sel[:, :], start=True, stop=False, skip_group_check=True)
            for d in range(1, NT):
                pe.matmul(ps[:, 7, d * E:NT * E], cbf[:, 1, :], sel[:, 0:(NT - d) * E], start=False, stop=(d == NT - 1), skip_group_check=True)
            for t in range(NT):
                mm = pe.matmul(ps[:, 6, 0:E], cbf[:, 1, :], sel[:, t * E:(t + 1) * E], start=(t == 0), stop=(t == NT - 1))
            mm.then_inc(rt_mm, 1)

            def tr_x(base):
                def fn(t, p, half):
                    pe.wait_ge(xg_loaded[p], 16 * (base // 2 + half + 1))
                    if base or type(t) is not int or t >= 2:
                        pe.wait_ge(x_lo, base + t - 1)
                    transposes(ps[:, p, :], xg[:, p, :], KT, x_tr)
                return fn

            def up(base, which):
                def fn(t, p, half):
                    a, need = which(t)
                    pe.wait_ge(x_lo, base + t + 1)
                    pe.wait_ge(h_ready, base + t)
                    pe.wait_ge(w_ready, need)
                    for m in range(2):
                        for k in range(KT):
                            c = (2 * k + m) * INTER
                            xh, xl = xhi[:, p, k * P:(k + 1) * P], xlo[:, p, k * P:(k + 1) * P]
                            wh, wl = whi[:, a, c:c + INTER], wlo[:, a, c:c + INTER]
                            pe.matmul(ps[:, 2 + m, 0:INTER], xh, wh, start=(k == 0), stop=False)
                            pe.matmul(ps[:, 2 + m, 0:INTER], xh, wl, start=False, stop=False)
                            mm = pe.matmul(ps[:, 2 + m, 0:INTER], xl, wh, start=False, stop=(k == KT - 1))
                    mm.then_inc(mm1, 1)
                return fn

            def down(base, which):
                def fn(t, p, half):
                    a, _ = which(t)
                    pe.wait_ge(h_lo, base + t + 1)
                    pe.wait_ge(y_out, base + t + 1)
                    for k in range(IC):
                        c = W13 + k * D
                        hh, hl = hhi[:, k * P:(k + 1) * P], hlo[:, k * P:(k + 1) * P]
                        wh, wl = whi[:, a, c:c + D], wlo[:, a, c:c + D]
                        pe.matmul(ps[:, 5 + p, :], hh, wh, start=(k == 0), stop=False)
                        pe.matmul(ps[:, 5 + p, :], hh, wl, start=False, stop=False)
                        mm = pe.matmul(ps[:, 5 + p, :], hl, wh, start=False, stop=(k == IC - 1))
                    mm.then_inc(mm2, 1)
                return fn

            def tr_h(base):
                def fn(t, p, half):
                    pe.wait_ge(h_ready, base + t + 1)
                    pe.wait_ge(h_lo, base + t)
                    transposes(ps[:, 4, :], hx[:, :], IC, h_tr)
                return fn

            def routed(t):
                a = pe.value_load(side[0:1, bass.ds(t, 1)], min_val=0, max_val=1)
                need = pe.value_load(order[0:1, bass.ds(t, 1)], min_val=2, max_val=E + 1)
                return bass.ds(a, 1), need

            def phase(base, tiles, which):
                pipeline(pe, tiles, [(0, up(base, which)), (1, tr_x(base)), (-1, down(base, which)), (0, tr_h(base))])

            pe.wait_ge(h_pad, 1)
            pe.wait_ge(rt_done, 1)
            phase(0, NT, lambda t: (0, 1))
            phase(NT, NR, routed)
            phase(NT + NR, NT, lambda t: (1, NW))

        @block.vector
        def _(dve):
            def norm_1(t, p, half):
                hold(dve, x_loaded[p], 16 * (half + 1))
                dve.bn_stats(st1[:, p, :], xin[:, p, :]).then_inc(s1_stats, 1)
                hold(dve, s1_stats, t + 1)
                dve.bn_aggr(mv1[:, p, :], st1[:, p, :]).then_inc(s1_aggr, 1)
                dve.wait_ge(s1_std, t + 1)
                dve.reciprocal(sd1[:, p, 1:2], sd1[:, p, 0:1]).then_inc(s1_rstd, 1)
                dve.wait_ge(s1_rstd, t + 1)
                dve.tensor_scalar(xin[:, p, :], xin[:, p, :], mv1[:, p, 0:1], sd1[:, p, 1:2], ALU.subtract, ALU.mult).then_inc(s1_xn, 1)

            def keep_1(t, p, half):
                dve.wait_ge(s1_xT, t + 1)
                dve.tensor_copy(xnT[:, :, bass.ds(t * P, P)], xT[:, p, :, :]).then_inc(s1_xnT, 1)

            pipeline(dve, NT, [(1, norm_1), (0, keep_1)])

            dve.wait_ge(w1_loaded, 32)

            def head(h, p, half):
                dve.wait_ge(g_mm, h + 1)
                dve.wait_ge(q_mm, B * h)
                dve.tensor_copy(g_sb[:, :], ps[:, 0, 0:HD]).then_inc(g_ready, 1)
                dve.wait_ge(s_mm, ST * h)
                for b in range(B):
                    dve.wait_ge(q_mm, B * h + b + 1)
                    dve.tensor_tensor(q_sb[:, b:b + 1, :], ps[:, 2 + b % 2:3 + b % 2, :], qdec[:, bass.ds(h, 1), :], ALU.mult).then_inc(q_ready, 1)
                for j in range(ST):
                    dve.wait_ge(s_abs, ST * h + j + 1)
                    blk = at_sb[:, AT_OFF[j]:AT_OFF[j] + S - P * j]
                    dve.tensor_scalar(blk, blk, 1.0, None, ALU.max).then_inc(at_max, 1)
                dve.wait_ge(o_ready, ST * h + ST)
                for t in range(NT):
                    st = dve.bn_stats(st3[:, t, bass.ds(h, 1), :], o_sb[:, t, bass.ds(h * HD, HD)])
                st.then_inc(o_stats, 1)

            for h in range(H):
                head(h, h % 2, h // 2)

            dve.wait_ge(o_stats, H)
            for t in range(NT):
                dve.bn_aggr(mv3[:, t, :], st3[:, t, :, :]).then_inc(o_aggr, 1)
            dve.wait_ge(o_std, 1)
            dve.reciprocal(sd3[:, 1, :], sd3[:, 0, :]).then_inc(o_rstd, 1)
            dve.wait_ge(o_rstd, 1)
            dve.wait_ge(w3_loaded, 48)

            def norm_o(t, p, half):
                dve.tensor_scalar(o_sb[:, bass.ds(t, 1), :], o_sb[:, bass.ds(t, 1), :], mv3[:, bass.ds(t, 1), 0],
                                  sd3[:, 1, bass.ds(t, 1)], ALU.subtract, ALU.mult).then_inc(o_normed, 1)

            def gate_o(t, p, half):
                dve.wait_ge(o_beta, t + 1)
                dve.wait_ge(gate_loaded[p], 16 * (half + 1))
                dve.tensor_tensor(gin[:, p:p + 1, :], gin[:, p:p + 1, :], o_sb[:, bass.ds(t, 1), :], ALU.mult).then_inc(gated, 1)

            def norm_x1(t, p, half):
                dve.wait_ge(a_mm, t + 1)
                dve.wait_ge(x3_loaded[p], 16 * (half + 1))
                dve.tensor_tensor(x1[:, bass.ds(t, 1), :], ps[:, 2 + p:3 + p, :], xin[:, p:p + 1, :], ALU.add).then_inc(x1_ready, 1)
                hold(dve, x1_ready, t + 1)
                dve.bn_stats(st1[:, p, :], x1[:, bass.ds(t, 1), :]).then_inc(l_stats, 1)
                hold(dve, l_stats, t + 1)
                dve.bn_aggr(mv1[:, p, :], st1[:, p, :]).then_inc(l_aggr, 1)
                dve.wait_ge(l_std, t + 1)
                dve.reciprocal(sd1[:, p, 1:2], sd1[:, p, 0:1]).then_inc(l_rstd, 1)
                dve.wait_ge(l_rstd, t + 1)
                if type(t) is not int or t >= 2:
                    dve.wait_ge(b_tr, t - 1)
                    dve.wait_ge(xn_stored[p], 16 * half)
                dve.tensor_scalar(xr[:, p:p + 1, :], x1[:, bass.ds(t, 1), :], mv1[:, p, 0:1], sd1[:, p, 1:2],
                                  ALU.subtract, ALU.mult).then_inc(xn_ready, 1)

            def keep_logits(t, p, half):
                dve.wait_ge(r_mm, t + 1)
                dve.tensor_copy(logits[:, bass.ds(t, 1), :], ps[:, 6 + p:7 + p, 0:E]).then_inc(r_ready, 1)

            pipeline(dve, NT, [(2, norm_o), (1, gate_o), (0, norm_x1), (-2, keep_logits)])

            steps = [0]

            def step(ins):
                steps[0] += 1
                ins.then_inc(rt, 1)
                dve.wait_ge(rt, steps[0])

            dve.wait_ge(r_ready, NT)
            for p in range(2):
                dve.wait_ge(xn_stored[p], 16 * (NT // 2))
            dve.memset(hx[:, :], 0.0).then_inc(h_pad, 1)
            step(dve.tensor_reduce(rmax[:, 0, :], logits[:, :, :], AX, ALU.max))
            step(dve.tensor_tensor(score[:, :, :], logits[:, :, :], rmax[:, 0, :, None].to_broadcast([P, NT, E]), ALU.subtract))
            dve.wait_ge(rt_exp, 1)
            step(dve.tensor_reduce(rmax[:, 0, :], score[:, :, :], AX, ALU.add))
            step(dve.reciprocal(rmax[:, 1, :], rmax[:, 0, :]))
            step(dve.tensor_tensor(score[:, :, :], score[:, :, :], rmax[:, 1, :, None].to_broadcast([P, NT, E]), ALU.mult))
            step(dve.tensor_reduce(gsc[:, :, :], score[:, :, :].rearrange("p t (g e) -> p (t g) e", g=G), AX, ALU.max))
            mine = gsc[:, :, :, None].to_broadcast([P, NT, G, G])
            other = gsc[:, :, None, :].to_broadcast([P, NT, G, G])
            beats = gcmp[:, 0, :, :]
            ties = gcmp[:, 1, :, :]
            step(dve.tensor_tensor(beats.rearrange("p t (g o) -> p t g o", g=G), other, mine, ALU.is_gt))
            step(dve.tensor_tensor(ties.rearrange("p t (g o) -> p t g o", g=G), other, mine, ALU.is_equal))
            step(dve.tensor_tensor(ties, ties, const[:, None, C_LG:C_LG + G * G].to_broadcast([P, NT, G * G]), ALU.mult))
            step(dve.tensor_tensor(beats, beats, ties, ALU.add))
            step(dve.tensor_reduce(gkeep[:, :, :], beats.rearrange("p t (g o) -> p (t g) o", g=G), AX, ALU.add))
            step(dve.tensor_scalar(gkeep[:, :, :], gkeep[:, :, :], TOPG - 0.5, -2.0, ALU.is_gt, ALU.mult))
            step(dve.tensor_tensor(masked[:, :, :].rearrange("p t (g e) -> p (t g) e", g=G),
                                   score[:, :, :].rearrange("p t (g e) -> p (t g) e", g=G),
                                   gkeep[:, :, :].rearrange("p t g -> p (t g)")[:, :, None].to_broadcast([P, NT * G, EG]), ALU.add))
            for t in range(NT):
                last = dve.max(top8[:, t, :], masked[:, t, :])
            step(last)
            for t in range(NT):
                last = dve.max_index(top8i[:, t, :], top8[:, t, :], masked[:, t, :])
            step(last)
            step(dve.tensor_copy(top8f[:, :, :], top8i[:, :, :]))
            hot = onehot[:, :, :].rearrange("p t (k e) -> p t k e", k=TOPK)
            step(dve.tensor_tensor(hot, top8f[:, :, 0:TOPK, None].to_broadcast([P, NT, TOPK, E]),
                                   const[:, None, None, C_IOTA:C_IOTA + E].to_broadcast([P, NT, TOPK, E]), ALU.is_equal))
            step(dve.tensor_reduce(self32[:, :, :], onehot[:, :, :].rearrange("p t (k e) -> p t e k", k=TOPK), AX, ALU.add))
            dve.tensor_copy(sel[:, :], self32[:, :, :].rearrange("p t e -> p (t e)")).then_inc(rt_sel, 1)
            dve.wait_ge(rt_mm, 1)
            tc = tcmp[:, :].rearrange("p (a b) -> p a b", a=E)
            step(dve.tensor_copy(ntile[:, 1, :], ps[:, 6, 0:E]))
            step(dve.tensor_tensor(tc, ntile[:, 1, :, None].to_broadcast([P, E, E]),
                                   const[:, None, C_CAP:C_CAP + E].to_broadcast([P, E, E]), ALU.is_gt))
            step(dve.tensor_reduce(ntile[:, 0, :], tc, AX, ALU.add))
            step(dve.tensor_tensor(tc, ntile[:, 0, None, :].to_broadcast([P, E, E]),
                                   const[:, C_LT:C_LT + E * E].rearrange("p (a b) -> p a b", a=E), ALU.mult))
            step(dve.tensor_reduce(ntile[:, 1, :], tc, AX, ALU.add))
            step(dve.scalar_tensor_tensor(slot[:, :].rearrange("p (t e) -> p t e", t=NT), ntile[:, 1, None, :].to_broadcast([P, NT, E]),
                                          float(P), ps[:, 7, 0:NT * E].rearrange("p (t e) -> p t e", t=NT), ALU.mult, ALU.add))
            step(dve.tensor_tensor(pick[:, :, :].rearrange("p t (k e) -> p t k e", k=TOPK), hot,
                                   slot[:, :].rearrange("p (t e) -> p t e", t=NT)[:, :, None, :].to_broadcast([P, NT, TOPK, E]), ALU.mult))
            step(dve.tensor_reduce(slotf[:, :], pick[:, :, :].rearrange("p t (k e) -> p (t k) e", k=TOPK), AX, ALU.add))
            step(dve.tensor_copy(sloti[:, :], slotf[:, :]))
            step(dve.tensor_tensor(ntile[0:1, 0, :], ntile[0:1, 0, :], ntile[0:1, 1, :], ALU.add))
            step(dve.tensor_tensor(ecmp[:, :, :], ntile[0:1, 0, None, :].to_broadcast([1, NR, E]),
                                   const[0:1, C_TILE:C_TILE + NR, None].to_broadcast([1, NR, E]), ALU.is_le))
            step(dve.tensor_reduce(tabf[:, 0:NR], ecmp[:, :, :], AX, ALU.add))
            step(dve.tensor_scalar(tabf[:, 0:NR], tabf[:, 0:NR], float(E - 1), 2.0, ALU.min, ALU.add))
            step(dve.tensor_scalar(tabf[:, NR:NR + E], ntile[0:1, 1, :], float(NT), None, ALU.add))
            step(dve.tensor_copy(order[:, :], tabf[:, :]))
            step(dve.tensor_scalar(side[:, :], order[:, 0:NR], 1, None, ALU.bitwise_and))
            dve.tensor_scalar(side[:, :], side[:, :], 1, None, ALU.bitwise_xor).then_inc(rt_done, 1)
            dve.wait_ge(rt_done, 1)

            def h_mult(base):
                def fn(t, p, half):
                    dve.wait_ge(silu, base + t + 1)
                    dve.wait_ge(h_tr, base + t)
                    dve.tensor_tensor(hx[:, 0:INTER], ps[:, 3, 0:INTER], sg[:, :], ALU.mult).then_inc(h_ready, 1)
                return fn

            def x_low(base):
                def fn(t, p, half):
                    dve.wait_ge(x_hi, base + t + 1)
                    dve.tensor_tensor(xlo[:, p, :], ps[:, p, :], xhi[:, p, :].bitcast(F32), ALU.subtract).then_inc(x_lo, 1)
                return fn

            def h_low(base):
                def fn(t, p, half):
                    dve.wait_ge(h_hi, base + t + 1)
                    dve.tensor_tensor(hlo[:, :], ps[:, 4, 0:IC * P], hhi[:, :].bitcast(F32), ALU.subtract).then_inc(h_lo, 1)
                return fn

            def add_shared(t, p, half):
                dve.wait_ge(mm2, t + 1)
                dve.tensor_tensor(x1[:, bass.ds(t, 1), :], x1[:, bass.ds(t, 1), :], ps[:, 5 + p:6 + p, :], ALU.add).then_inc(y_out, 1)

            def combine(t, p, half):
                dve.wait_ge(mm2, NT + NR + t + 1)
                if type(t) is not int or t >= 2:
                    dve.wait_ge(out_stored[p], 16 * half)
                dve.tensor_tensor(osb[:, p:p + 1, :], x1[:, bass.ds(t, 1), :], ps[:, 5 + p:6 + p, :], ALU.add).then_inc(y_out, 1)
                dve.wait_ge(y_out, 2 + NT + NR + t + 1)
                dve.sem_inc(comb, 1)
                dve.wait_ge(gathered[p], 16 * TOPK * (half + 1))
                for k in range(TOPK):
                    dve.wait_ge(comb, (1 + TOPK) * t + k + 1)
                    dve.scalar_tensor_tensor(osb[:, p, :], gath[:, p, k, :], top8[:, bass.ds(t, 1), k], osb[:, p, :],
                                             ALU.mult, ALU.add).then_inc(comb, 1)

            pipeline(dve, NT, [(0, h_mult(0)), (1, x_low(0)), (-1, add_shared), (0, h_low(0))])
            pipeline(dve, NR, [(0, h_mult(NT)), (1, x_low(NT)), (0, h_low(NT))])
            pipeline(dve, NT, [(0, h_mult(NT + NR)), (1, x_low(NT + NR)), (0, h_low(NT + NR)), (-1, combine)])


def constants():
    import numpy as np
    c = np.zeros((P, C_ALL), np.float32)
    r = np.arange(P)
    c[:, C_ID:C_ID + P] = np.eye(P)
    c[:, C_UP:C_UP + P] = r[:, None] < r[None, :]
    c[:, C_ONE:C_ONE + P] = 1.0
    e = np.arange(E)
    c[:, C_IOTA:C_IOTA + E] = e
    c[:, C_CAP:C_CAP + E] = P * e
    c[:, C_LT:C_LT + E * E] = (e[None, :] < e[:, None]).reshape(-1)
    g = np.arange(G)
    c[:, C_LG:C_LG + G * G] = (g[None, :] < g[:, None]).reshape(-1)
    c[:, C_TILE:C_TILE + NR] = np.arange(NR)
    c[:, C_EPS] = LN_EPS
    c[:, C_EPS + 1] = GN_EPS
    gam = 1.0 - 2.0 ** (-5.0 - np.arange(H, dtype=np.float64))
    query = gam[:, None] ** -np.arange(S, dtype=np.float64)[None, :]
    key = 1.0 / query / np.sqrt(np.cumsum(query, axis=1)) / np.sqrt(float(HD))
    c[:, C_KDEC:C_KDEC + H * ST] = key.reshape(H * ST, P).T
    return c, query.astype(np.float32)


def kernel(**inputs):
    import numpy as np
    import concourse.bacc as bacc
    from concourse.bass_utils import run_bass_kernel_spmd as run

    x = np.ascontiguousarray(inputs["x"]).reshape(TOK, D)
    ctxT = np.ascontiguousarray(inputs["ctx_2048"]).reshape(TOK, D).T.reshape(H, HD, TOK)
    wh = np.ascontiguousarray(inputs["L0_xattn_Wh"])
    heads = np.concatenate([ctxT, wh, wh.transpose(0, 2, 1)], axis=2)
    gn = np.stack([inputs["L0_xattn_gn_gamma"], inputs["L0_xattn_gn_beta"]])

    def pieces(w1, w3, w2):
        up = np.stack([w1.T.reshape(KT, P, INTER), w3.T.reshape(KT, P, INTER)], axis=2)
        down = np.zeros((IC * P, D), w2.dtype)
        down[:INTER] = w2.T
        return np.concatenate([up.transpose(1, 0, 2, 3).reshape(P, W13),
                               down.reshape(IC, P, D).transpose(1, 0, 2).reshape(P, IC * D)], axis=1)

    w1, w3, w2 = (np.asarray(inputs[f"L0_ffn_W{n}"]) for n in (1, 3, 2))
    s1, s3, s2 = (np.asarray(inputs[f"L0_ffn_Ws{n}"]) for n in (1, 3, 2))
    shared = [pieces(s1[i * INTER:(i + 1) * INTER], s3[i * INTER:(i + 1) * INTER], s2[:, i * INTER:(i + 1) * INTER])
              for i in range(N_SHARED)]
    wexp = np.stack([shared[0]] + [pieces(w1[e], w3[e], w2[e]) for e in range(E)] + [shared[1]])
    tables, qdecay = constants()

    arrays = {"x_in": x, "heads_in": heads, "wg_in": inputs["L0_xattn_wg_w"], "wo_in": inputs["L0_xattn_wo_w"],
              "gn_in": gn, "router_in": np.asarray(inputs["L0_ffn_Wg"]).T, "wexp_in": wexp,
              "tables_in": tables, "qdecay_in": qdecay}
    arrays = {n: np.ascontiguousarray(a) for n, a in arrays.items()}
    nc = bacc.Bacc("TRN2", target_bir_lowering=False, num_devices=1)
    aps = [nc.dram_tensor(n, a.shape, mybir.dt.from_np(a.dtype), kind="ExternalInput").ap() for n, a in arrays.items()]
    out = nc.dram_tensor("y_out", (B, S, D), F32, kind="ExternalOutput").ap()
    xattn_moe(nc, *aps, out.rearrange("b s d -> (b s) d"))
    r = run(nc, [arrays], core_ids=[0])
    return r.results[0]["y_out"]
```

```python
from contextlib import ExitStack

import concourse.bass as bass
from concourse import mybir

ALU = mybir.AluOpType
ACT = mybir.ActivationFunctionType
F32 = mybir.dt.float32
F32R = mybir.dt.float32r
BF16 = mybir.dt.bfloat16
I32 = mybir.dt.int32
U32 = mybir.dt.uint32
AX = mybir.AxisListType.X

P = 128
B, S, D = 4, 512, 512
H, HD = 4, 128
KT = D // P
ST = S // P
TOK = B * S
NT = TOK // P
E, G, TOPG, TOPK = 16, 4, 2, 4
EG = E // G
INTER = 352
IC = 3
N_SHARED = 2
XR = 4
XG = 4
GR = 4
NW = E + N_SHARED
W13 = KT * 2 * INTER
WCOL = W13 + IC * D
NR = TOK * TOPK // P + E
PIECE = 2 * WCOL // NT
LN_EPS, GN_EPS = 1e-5, 1e-3
SENTINEL = -9.0

C_ID, C_UP, C_ONE = 0, 128, 256
C_IOTA, C_CAP, C_LT, C_LG, C_TILE, C_KDEC = 384, 400, 416, 672, 688, 768
C_EPS = 784
C_ALL = 786
HC_W, HC_WT = TOK, TOK + HD
HCOL = TOK + 2 * HD
AT_OFF = [0, 512, 896, 1152]
AT_COL = 1280


def pipeline(eng, tiles, parts, ramp=2, ring=2, each_pass=None):
    most = max(a for a, _ in parts)
    least = min(a for a, _ in parts)
    lo = min(max(0, ramp - least), tiles)
    hi = max(lo, tiles - max(0, most))
    hi -= (hi - lo) % ring

    def peeled(s):
        for ahead, fn in parts:
            t = s + ahead
            if 0 <= t < tiles:
                fn(t, t % ring, t // ring)

    for s in range(-max(0, most), lo):
        peeled(s)
    with eng.Fori(0, (hi - lo) // ring) as j:
        if each_pass:
            each_pass(j)
        for u in range(ring):
            for ahead, fn in parts:
                t = lo + u + ahead
                fn(ring * j + t, t % ring, j + t // ring)
    for s in range(hi, tiles - min(0, least)):
        peeled(s)


def xattn_moe(nc, x, heads, wg, wo, gn, wr, wexp, tables, qdecay, out):
    outer = ExitStack()
    with outer:
        def psum(name, shape, dt):
            return outer.enter_context(nc.psum_tensor(name, shape, dt))

        def sem(name):
            return outer.enter_context(nc.semaphore(name))

        def keep(name, shape, dt):
            return outer.enter_context(nc.sbuf_tensor(name, shape, dt))

        const = keep("const", [P, C_ALL], F32)
        cbf = keep("cbf", [P, 2, P], BF16)
        res = keep("res", [P, NT * D], F32)
        xnT = res[:, :].rearrange("p (h n) -> p h n", h=H)
        x1 = res[:, :].rearrange("p (t n) -> p t n", t=NT)
        raw = keep("raw", [P, 2, WCOL], F32)
        logits = keep("logits", [P, NT, E], F32)
        ident = const[:, C_ID:C_ID + P]
        ones = const[:, C_ONE:C_ONE + P]

        with ExitStack() as early:
            def sb1(name, shape, dt):
                return early.enter_context(nc.sbuf_tensor(name, shape, dt))
            head_in = sb1("head_in", [P, 2, HCOL], F32)
            v_sb = sb1("v_sb", [P, ST, B * HD], F32)
            q_sb = sb1("q_sb", [P, B, S], F32)
            at_sb = sb1("at_sb", [P, AT_COL], F32)
            g_sb = sb1("g_sb", [P, HD], F32)
            wg_sb = sb1("wg_sb", [P, KT, D], F32)
            qdec = sb1("qdec", [P, H, S], F32)
            xq = sb1("xq", [P, XR, D], F32)
            gate_out = sb1("gate_out", [P, 2, D], F32)
        whi = keep("whi", [P, 2, WCOL], F32R)
        wlo = keep("wlo", [P, 2, WCOL], F32R)
        raw_all, whi_all, wlo_all = (w[:, :, :].rearrange("p a n -> p (a n)") for w in (raw, whi, wlo))

        with ExitStack() as mid:
            def sb2(name, shape, dt):
                return mid.enter_context(nc.sbuf_tensor(name, shape, dt))
            o_sb = sb2("o_sb", [P, NT, D], F32)
            xin = sb2("xin", [P, 2, D], F32)
            gin = sb2("gin", [P, 2, D], F32)
            xr = sb2("xr", [P, 2, D], F32)
            xT = sb2("xT", [P, 2, KT, P], F32)
            xT2 = sb2("xT2", [P, 2, KT, P], F32)
            wo_sb = sb2("wo_sb", [P, KT, D], F32)
            gn_sb = sb2("gn_sb", [P, 2, D], F32)
            wr_sb = sb2("wr_sb", [P, KT, E], F32)
            zero = sb2("zero", [P, D], F32)
            st1 = sb2("st1", [P, 2, 6], F32)
            mv1 = sb2("mv1", [P, 2, 2], F32)
            sd1 = sb2("sd1", [P, 2, 2], F32)
            st3 = sb2("st3", [P, NT, H, 6], F32)
            mv3 = sb2("mv3", [P, NT, 2], F32)
            sd3 = sb2("sd3", [P, 2, NT], F32)

        def sb3(name, shape, dt):
            return keep(name, shape, dt)
        xg = sb3("xg", [P, XG, D], F32)
        xhi = sb3("xhi", [P, 2, KT * P], F32R)
        xlo = sb3("xlo", [P, 2, KT * P], F32R)
        sg = sb3("sg", [P, INTER], F32)
        hx = sb3("hx", [P, IC * P], F32)
        hhi = sb3("hhi", [P, IC * P], F32R)
        hlo = sb3("hlo", [P, IC * P], F32R)
        ysb = sb3("ysb", [P, 2, D], F32)
        scat = sb3("scat", [P, XR, D], F32)
        gath = raw[:, :, :].rearrange("p a n -> p (a n)")[:, 0:GR * TOPK * D].rearrange("p (r k n) -> p r k n", r=GR, k=TOPK)
        osb = sb3("osb", [P, 2, D], F32)
        rmax = sb3("rmax", [P, 2, NT], F32)
        score = sb3("score", [P, NT, E], F32)
        gsc = sb3("gsc", [P, NT, G], F32)
        gcmp = sb3("gcmp", [P, 2, NT, G * G], F32)
        gkeep = sb3("gkeep", [P, NT, G], F32)
        masked = sb3("masked", [P, NT, E], F32)
        top8 = sb3("top8", [P, NT, 8], F32)
        top8i = sb3("top8i", [P, NT, 8], U32)
        top8f = sb3("top8f", [P, NT, 8], F32)
        onehot = sb3("onehot", [P, NT, TOPK * E], F32)
        sel = sb3("sel", [P, NT * E], BF16)
        self32 = sb3("self32", [P, NT, E], F32)
        tcmp = sb3("tcmp", [P, E * E], F32)
        ntile = sb3("ntile", [P, 2, E], F32)
        slot = sb3("slot", [P, NT * E], F32)
        pick = sb3("pick", [P, NT, TOPK * E], F32)
        slotf = sb3("slotf", [P, NT * TOPK], F32)
        sloti = sb3("sloti", [P, NT * TOPK], I32)
        slotc = sb3("slotc", [P, XR, TOPK], I32)
        ecmp = sb3("ecmp", [1, NR, E], F32)
        tabf = sb3("tabf", [1, NR + E], F32)
        order = sb3("order", [1, NR + E], I32)
        packf = sb3("packf", [1, (NR - 4) // 2], F32)
        packed = sb3("packed", [1, (NR - 4) // 2], I32)

        ps = psum("ps", [P, 8, 512], F32)

        gate_d = nc.dram_tensor("gate_d", [TOK, D], F32, kind="Internal").ap()
        xn_d = nc.dram_tensor("xn_d", [TOK, D], F32, kind="Internal").ap()
        xslot_d = nc.dram_tensor("xslot_d", [NR * P, D], F32, kind="Internal").ap()
        yslot_d = nc.dram_tensor("yslot_d", [NR * P, D], F32, kind="Internal").ap()

        qdec_loaded = sem("qdec_loaded")
        c_loaded, w1_loaded, w3_loaded = sem("c_loaded"), sem("w1_loaded"), sem("w3_loaded")
        x_loaded = [sem(f"x_loaded{r}") for r in range(XR)]
        cbf_ready, zero_ready, zeroed = sem("cbf_ready"), sem("zero_ready"), sem("zeroed")
        s1_stats, s1_aggr, s1_std, s1_rstd, s1_xn = (sem(f"s1_{n}") for n in ("stats", "aggr", "std", "rstd", "xn"))
        s1_tr = sem("s1_tr")
        s1_xT, s1_xnT = sem("s1_xT"), sem("s1_xnT")
        s1_mm = sem("s1_mm")
        s1_gate = sem("s1_gate")
        gate_stored = [sem(f"gate_stored{p}") for p in range(2)]
        head_loaded = [sem(f"head_loaded{p}") for p in range(2)]
        g_mm, g_ready, v_mm, v_ready, q_mm, q_ready = (sem(n) for n in ("g_mm", "g_ready", "v_mm", "v_ready", "q_mm", "q_ready"))
        s_mm, s_abs, at_max, at_ready, o_mm, o_ready = (sem(n) for n in ("s_mm", "s_abs", "at_max", "at_ready", "o_mm", "o_ready"))
        o_stats, o_aggr, o_std, o_rstd = (sem(n) for n in ("o_stats", "o_aggr", "o_std", "o_rstd"))
        gate_loaded = [sem(f"gate_loaded{p}") for p in range(2)]
        x3_loaded = [sem(f"x3_loaded{p}") for p in range(2)]
        o_normed, o_gamma, o_beta, gated = (sem(n) for n in ("o_normed", "o_gamma", "o_beta", "gated"))
        a_tr, a_xT, a_mm = (sem(n) for n in ("a_tr", "a_xT", "a_mm"))
        x1_ready, l_stats, l_aggr, l_std, l_rstd, xn_ready = (sem(n) for n in ("x1_ready", "l_stats", "l_aggr", "l_std", "l_rstd", "xn_ready"))
        b_tr, b_xT, r_mm, r_ready = (sem(n) for n in ("b_tr", "b_xT", "r_mm", "r_ready"))
        xn_stored = [sem(f"xn_stored{p}") for p in range(2)]
        rt, rt_exp, rt_sel, rt_mm, rt_slots, rt_done = (sem(n) for n in ("rt", "rt_exp", "rt_sel", "rt_mm", "rt_slots", "rt_done"))
        raw_loaded = [sem(f"raw_loaded{p}") for p in range(2)]
        first_hi, first_lo, w_hi = (sem(n) for n in ("first_hi", "first_lo", "w_hi"))
        w13_ready, w2_ready = sem("w13_ready"), sem("w2_ready")
        xg_loaded = [sem(f"xg_loaded{r}") for r in range(XG)]
        x_tr = sem("x_tr")
        x_hi, x_lo = sem("x_hi"), sem("x_lo")
        mm1 = sem("mm1")
        silu, h_ready, h_tr, h_hi, h_lo, h_pad = (sem(n) for n in ("silu", "h_ready", "h_tr", "h_hi", "h_lo", "h_pad"))
        mm2 = sem("mm2")
        y_out = sem("y_out")
        y_stored = [sem(f"y_stored{p}") for p in range(2)]
        scat_loaded = [sem(f"scat_loaded{r}") for r in range(XR)]
        scattered = [sem(f"scattered{r}") for r in range(XR)]
        slotc_ready = sem("slotc_ready")
        gathered = [sem(f"gathered{r}") for r in range(GR)]
        comb = sem("comb")
        out_stored = [sem(f"out_stored{p}") for p in range(2)]

        block = outer.enter_context(nc.Block())

        def hold(eng, sem, value):
            if type(value) is not int:
                value = eng.snap(eng.to_reg(value))
            eng.wait_ge(c_loaded, 16)
            eng.wait_ge(sem, value)

        def rows(dram, t):
            return dram[bass.ds(t * P, P), :]

        @block.sync
        def _(sp):
            sp.dma_start(const[:, :], tables).then_inc(c_loaded, 16)
            sp.dma_start(wg_sb[:, :, :], wg.rearrange("(k p) n -> p k n", p=P)).then_inc(w1_loaded, 16)

            def load_x(t, r, turn):
                sp.wait_ge(s1_tr, t + 1)
                sp.dma_start(xq[:, r, :], rows(x, t)).then_inc(x_loaded[r], 16)

            def store_gate(t, r, turn):
                p = r % 2
                sp.wait_ge(s1_gate, 2 + t + 1)
                sp.dma_start(rows(gate_d, t), gate_out[:, p, :]).then_inc(gate_stored[p], 16)

            pipeline(sp, NT, [(3, load_x), (-1, store_gate)], ring=XR)
            sp.dma_start(wo_sb[:, :, :], wo.rearrange("(k p) n -> p k n", p=P)).then_inc(w3_loaded, 16)
            sp.dma_start(gn_sb[:, :, :], gn[None, :, :].to_broadcast([P, 2, D])).then_inc(w3_loaded, 16)
            sp.dma_start(wr_sb[:, :, :], wr.rearrange("(k p) n -> p k n", p=P)).then_inc(w3_loaded, 16)
            sp.wait_ge(zero_ready, 1)
            for c in range(NR // 8):
                sp.dma_start(xslot_d[c * 8 * P:(c + 1) * 8 * P, :].rearrange("(p r) n -> p r n", p=P),
                             zero[:, None, :].to_broadcast([P, 8, D])).then_inc(zeroed, 16)

            for p in range(2):
                sp.wait_ge(gate_stored[p], 16 * (NT // 2))

            def load_gate(t, p, half):
                if type(t) is not int or t >= 2:
                    sp.wait_ge(a_tr, t - 1)
                sp.dma_start(gin[:, p, :], rows(gate_d, t)).then_inc(gate_loaded[p], 16)

            def load_x3(t, p, half):
                if type(t) is not int or t >= 2:
                    sp.wait_ge(x1_ready, t - 1)
                sp.dma_start(xin[:, p, :], rows(x, t)).then_inc(x3_loaded[p], 16)

            def store_xn(t, p, half):
                sp.wait_ge(xn_ready, t + 1)
                sp.dma_start(rows(xn_d, t), xr[:, p, :]).then_inc(xn_stored[p], 16)

            pipeline(sp, NT, [(2, load_gate), (-1, store_xn), (1, load_x3)])

            for p in range(2):
                sp.wait_ge(xn_stored[p], 16 * (NT // 2))
            sp.wait_ge(r_ready, NT)

            def load_tile(base, src):
                def fn(t, r, turn):
                    sp.wait_ge(x_tr, base + t + 1)
                    sp.dma_start(xg[:, r, :], rows(src, t)).then_inc(xg_loaded[r], 16)
                return fn

            def store_y(t, r, turn):
                p = r % 2
                sp.wait_ge(y_out, 2 + NT + t + 1)
                sp.dma_start(rows(yslot_d, t), ysb[:, p, :]).then_inc(y_stored[p], 16)

            def store_out(t, r, turn):
                p = r % 2
                sp.wait_ge(comb, TOPK * (t + 1))
                sp.dma_start(rows(out, t), osb[:, p, :]).then_inc(out_stored[p], 16)

            pipeline(sp, NT, [(XG, load_tile(0, xn_d))], ring=XG)
            for r in range(XR):
                sp.wait_ge(scattered[r], 16 * TOPK * (NT // XR))
            pipeline(sp, NR, [(XG, load_tile(NT, xslot_d)), (-1, store_y)], ring=XG)
            pipeline(sp, NT, [(XG, load_tile(NT + NR, xn_d)), (-5, store_out)], ring=XG)
            for p in range(2):
                sp.wait_ge(out_stored[p], 16 * (NT // 2))

        @block.gpsimd
        def _(pool):
            def load_head(h):
                if h >= 2:
                    pool.wait_ge(s_mm, ST * (h - 1))
                pool.dma_start(head_in[:, h % 2, :], heads[h, :, :]).then_inc(head_loaded[h % 2], 16)

            pool.memset(zero[:, :], 0.0).then_inc(zero_ready, 1)
            pool.wait_ge(c_loaded, 16)
            pool.tensor_copy(cbf[:, :, :], const[:, C_UP:C_UP + 2 * P].rearrange("p (a n) -> p a n", a=2)).then_inc(cbf_ready, 1)

            for h in range(2):
                pool.wait_ge(s1_tr, XR + 1 + 4 * h)
                load_head(h)
            pool.dma_start(qdec[:, :, :], qdecay[None, :, :].to_broadcast([P, H, S])).then_inc(qdec_loaded, 16)
            pool.wait_ge(s1_tr, XR + NT)
            for p in range(2):
                pool.dma_start(raw[:, p, :], wexp[p, :, :]).then_inc(raw_loaded[p], 16)

            def diagonals(h, p, half):
                for j in range(ST):
                    pool.wait_ge(at_max, ST * h + j + 1)
                    blk = at_sb[:, AT_OFF[j]:AT_OFF[j] + P]
                    pool.affine_select(out=blk, in_=blk, compare_op=ALU.is_ge, fill=1.0, base=0,
                                       pattern=[[1, P]], channel_multiplier=-1).then_inc(at_ready, 1)

            for h in range(H):
                diagonals(h, h % 2, h // 2)
                if h + 2 < H:
                    load_head(h + 2)

            def split(o, p, half, before):
                up, down = slice(0, W13), slice(W13, WCOL)
                hold(pool, raw_loaded[p], 16 * (half + 1))
                hold(pool, mm1, 2 + before)
                pool.tensor_copy(whi[:, p, up], raw[:, p, up]).then_inc(w_hi, 1)
                hold(pool, w_hi, 2 * o - 3)
                pool.tensor_tensor(wlo[:, p, up], raw[:, p, up], whi[:, p, up].bitcast(F32), ALU.subtract).then_inc(w13_ready, 1)
                hold(pool, mm2, before)
                pool.tensor_copy(whi[:, p, down], raw[:, p, down]).then_inc(w_hi, 1)
                hold(pool, w_hi, 2 * o - 2)
                pool.tensor_tensor(wlo[:, p, down], raw[:, p, down], whi[:, p, down].bitcast(F32), ALU.subtract).then_inc(w2_ready, 1)

            def next_raw(o, p):
                hold(pool, w13_ready, o + 1)
                hold(pool, w2_ready, o + 1)
                pool.dma_start(raw[:, p, :], wexp[bass.ds(o + 2, 1), :, :].rearrange("a p n -> p (a n)")).then_inc(raw_loaded[p], 16)

            def affine(t, p, half):
                hold(pool, o_normed, t + 1)
                pool.tensor_tensor(o_sb[:, bass.ds(t, 1), :], o_sb[:, bass.ds(t, 1), :], gn_sb[:, 0:1, :], ALU.mult).then_inc(o_gamma, 1)
                hold(pool, o_gamma, t + 1)
                pool.tensor_tensor(o_sb[:, bass.ds(t, 1), :], o_sb[:, bass.ds(t, 1), :], gn_sb[:, 1:2, :], ALU.add).then_inc(o_beta, 1)

            pool.wait_ge(w3_loaded, 48)
            pipeline(pool, NT, [(0, affine)], ramp=0)

            for o in range(2):
                pool.wait_ge(first_lo, NT)
                pool.dma_start(raw[:, o, :], wexp[o + 2, :, :]).then_inc(raw_loaded[o], 16)

            pool.wait_ge(rt_slots, 1)
            pool.wait_ge(zeroed, 16 * (NR // 8))

            def load_scat(t, r, turn):
                if type(t) is not int or t >= XR:
                    hold(pool, scattered[r], 16 * TOPK * turn)
                pool.dma_start(scat[:, r, :], rows(xn_d, t)).then_inc(scat_loaded[r], 16)
                pool.tensor_copy(slotc[:, r, :], sloti[:, bass.ds(t * TOPK, TOPK)]).then_inc(slotc_ready, 1)

            def scatter(t, r, turn):
                hold(pool, scat_loaded[r], 16 * (turn + 1))
                hold(pool, slotc_ready, t + 1)
                for k in range(TOPK):
                    pool.indirect_dma_start(
                        out=xslot_d, out_offset=bass.IndirectOffsetOnAxis(ap=slotc[:, r, k:k + 1], axis=0),
                        in_=scat[:, r, :], in_offset=None).then_inc(scattered[r], 16)

            pipeline(pool, NT, [(2, load_scat), (0, scatter)], ramp=XR, ring=XR)

            pool.wait_ge(rt_done, 1)
            def tiles_through(o):
                return pool.value_load(order[0:1, bass.ds(o + NR - 2, 1)], min_val=NT, max_val=NT + NR)

            def set_and_next(o, p, half):
                split(o + 2, p, half + 1, tiles_through(o + 2))
                next_raw(o + 2, p)

            pipeline(pool, NW - 4, [(0, set_and_next)], ramp=0)
            for o in range(NW - 2, NW):
                split(o, o % 2, o // 2, tiles_through(o))

            for p in range(2):
                pool.wait_ge(y_stored[p], 16 * (NR // 2))

            def gather(t, r, turn):
                if type(t) is not int or t >= GR:
                    hold(pool, comb, TOPK * (t - GR + 1))
                pool.tensor_copy(slotc[:, r, :], sloti[:, bass.ds(t * TOPK, TOPK)]).then_inc(slotc_ready, 1)
                hold(pool, slotc_ready, NT + t + 1)
                for k in range(TOPK):
                    pool.indirect_dma_start(
                        out=gath[:, r, k, :], out_offset=None, in_=yslot_d,
                        in_offset=bass.IndirectOffsetOnAxis(ap=slotc[:, r, k:k + 1], axis=0)).then_inc(gathered[r], 16)

            pipeline(pool, NT, [(0, gather)], ramp=GR, ring=GR)

        @block.scalar
        def _(act):
            act.sem_inc(s1_gate, 2)
            act.sem_inc(y_out, 2)
            act.wait_ge(c_loaded, 16)

            def std_1(t, p, half):
                act.wait_ge(s1_aggr, t + 1)
                act.activation(sd1[:, p, 0:1], mv1[:, p, 1:2], ACT.Sqrt, bias=const[:, C_EPS:C_EPS + 1]).then_inc(s1_std, 1)

            def evac_1(t, p, half):
                act.wait_ge(s1_tr, XR + t + 1)
                act.wait_ge(s1_mm, t + 1)
                act.wait_ge(s1_xnT, t)
                act.activation(xT[:, p, :, :], ps[:, p, :], ACT.Copy).then_inc(s1_xT, 1)

            def relu_1(t, p, half):
                act.wait_ge(s1_mm, 2 + t + 1)
                if type(t) is not int or t >= 2:
                    act.wait_ge(gate_stored[p], 16 * half)
                act.activation(gate_out[:, p, :], ps[:, 2 + p, :], ACT.Relu).then_inc(s1_gate, 1)

            pipeline(act, NT, [(2, std_1), (0, evac_1), (-1, relu_1)])

            def head(h, p, half):
                act.wait_ge(o_mm, ST * h)
                for tt in range(ST):
                    act.wait_ge(v_mm, ST * h + tt + 1)
                    act.activation(v_sb[:, tt, :], ps[:, (1 + tt) % 2, :], ACT.Copy).then_inc(v_ready, 1)
                for j in range(ST):
                    act.wait_ge(s_mm, ST * h + j + 1)
                    n = S - P * j
                    act.activation(at_sb[:, AT_OFF[j]:AT_OFF[j] + n], ps[:, 4 + j % 2, 0:n], ACT.Abs,
                                   scale=const[:, bass.ds(C_KDEC + h * ST + j, 1)]).then_inc(s_abs, 1)
                for i in range(ST):
                    act.wait_ge(o_mm, ST * h + i + 1)
                    act.activation(o_sb[:, :, :].rearrange("p (b i) n -> p b i n", i=ST)[:, :, i, bass.ds(h * HD, HD)],
                                   ps[:, 6 + i % 2, :].rearrange("p (b n) -> p b n", b=B), ACT.Copy).then_inc(o_ready, 1)

            for h in range(H):
                head(h, h % 2, h // 2)

            act.wait_ge(o_aggr, NT)
            act.activation(sd3[:, 0, :], mv3[:, :, 1], ACT.Sqrt, bias=const[:, C_EPS + 1:C_EPS + 2]).then_inc(o_std, 1)
            act.wait_ge(o_mm, ST * H)
            for p in range(2):
                act.wait_ge(gate_stored[p], 16 * (NT // 2))
                act.wait_ge(raw_loaded[p], 16)

            def first_high(t, p, half):
                act.activation(whi_all[:, bass.ds(t * PIECE, PIECE)], raw_all[:, bass.ds(t * PIECE, PIECE)], ACT.Copy).then_inc(first_hi, 1)

            def evac_a(t, p, half):
                act.wait_ge(a_tr, t + 1)
                if type(t) is not int or t >= 2:
                    act.wait_ge(a_mm, t - 1)
                act.activation(xT[:, p, :, :], ps[:, p, :], ACT.Copy).then_inc(a_xT, 1)

            def evac_b(t, p, half):
                act.wait_ge(b_tr, t + 1)
                if type(t) is not int or t >= 2:
                    act.wait_ge(r_mm, t - 1)
                act.activation(xT2[:, p, :, :], ps[:, 4 + p, :], ACT.Copy).then_inc(b_xT, 1)

            def std_3(t, p, half):
                act.wait_ge(l_aggr, t + 1)
                act.activation(sd1[:, p, 0:1], mv1[:, p, 1:2], ACT.Sqrt, bias=const[:, C_EPS:C_EPS + 1]).then_inc(l_std, 1)

            pipeline(act, NT, [(1, evac_a), (-1, evac_b), (0, std_3), (0, first_high)])

            act.wait_ge(rt, 2)
            act.activation(score[:, :, :], score[:, :, :], ACT.Exp).then_inc(rt_exp, 1)

            def silu_g(base):
                def fn(t, p, half):
                    act.wait_ge(mm1, 2 + base + t + 1)
                    act.wait_ge(h_ready, base + t)
                    act.activation(sg[:, :], ps[:, 2, 0:INTER], ACT.Silu).then_inc(silu, 1)
                return fn

            def x_high(base):
                def fn(t, p, half):
                    act.wait_ge(x_tr, XG + base + t + 1)
                    act.wait_ge(mm1, base + t + 1)
                    act.activation(xhi[:, p, :], ps[:, p, :], ACT.Copy).then_inc(x_hi, 1)
                return fn

            def h_high(base):
                def fn(t, p, half):
                    act.wait_ge(h_tr, base + t + 1)
                    act.wait_ge(mm2, base + t)
                    act.activation(hhi[:, :], ps[:, 4, 0:IC * P], ACT.Copy).then_inc(h_hi, 1)
                return fn

            def y_evac(t, p, half):
                act.wait_ge(mm2, NT + t + 1)
                if type(t) is not int or t >= 2:
                    act.wait_ge(y_stored[p], 16 * half)
                act.activation(ysb[:, p, :], ps[:, 5 + p, :], ACT.Copy).then_inc(y_out, 1)

            pipeline(act, NT, [(0, silu_g(0)), (1, x_high(0)), (0, h_high(0))])
            pipeline(act, NR, [(0, silu_g(NT)), (1, x_high(NT)), (-1, y_evac), (0, h_high(NT))])
            pipeline(act, NT, [(0, silu_g(NT + NR)), (1, x_high(NT + NR)), (0, h_high(NT + NR))])

        @block.tensor
        def _(pe):
            pe.sem_inc(s1_tr, XR)
            pe.sem_inc(s1_mm, 2)
            pe.sem_inc(x_tr, XG)
            pe.sem_inc(mm1, 2)
            pe.wait_ge(c_loaded, 16)

            def transposes(dst, src, n, done):
                for k in range(n):
                    mm = pe.transpose(dst[:, k * P:(k + 1) * P], src[:, k * P:(k + 1) * P], ident)
                mm.then_inc(done, 1)

            def tr_1(t, r, turn):
                p = r % 2
                pe.wait_ge(s1_xn, t + 1)
                if type(t) is not int or t >= 2:
                    pe.wait_ge(s1_xT, t - 1)
                transposes(ps[:, p, :], xq[:, r, :], KT, s1_tr)

            def gate_1(t, r, turn):
                p = r % 2
                pe.wait_ge(s1_xT, t + 1)
                pe.wait_ge(s1_gate, t + 1)
                for k in range(KT):
                    mm = pe.matmul(ps[:, 2 + p, :], xT[:, p, k, :], wg_sb[:, k, :], start=(k == 0), stop=(k == KT - 1))
                mm.then_inc(s1_mm, 1)

            pe.wait_ge(w1_loaded, 16)
            pipeline(pe, NT, [(1, tr_1), (0, gate_1)], ring=XR)

            pe.wait_ge(s1_gate, 2 + NT)
            pe.wait_ge(s1_xnT, NT)

            def head(h, p, half):
                ctxT = head_in[:, p, 0:TOK]
                w = head_in[:, p, HC_W:HC_W + HD]
                wT = head_in[:, p, HC_WT:HC_WT + HD]
                pe.wait_ge(head_loaded[p], 16 * (half + 1))
                pe.wait_ge(v_ready, ST * h)
                pe.matmul(ps[:, 0, 0:HD], wT, wT, start=True, stop=True).then_inc(g_mm, 1)
                for tt in range(ST):
                    if tt == 1:
                        pe.wait_ge(g_ready, h + 1)
                    if tt >= 2:
                        pe.wait_ge(v_ready, ST * h + tt - 1)
                    for b in range(B):
                        mm = pe.matmul(ps[:, (1 + tt) % 2, b * HD:(b + 1) * HD], ctxT[:, b * S + tt * P:b * S + (tt + 1) * P], w,
                                       start=True, stop=True)
                    mm.then_inc(v_mm, 1)
                for b in range(B):
                    pe.wait_ge(q_ready, B * h + max(b - 1, 0))
                    pe.matmul(ps[:, 2 + b % 2, :], g_sb[:, :], xnT[:, bass.ds(h, 1), b * S:(b + 1) * S],
                              start=True, stop=True).then_inc(q_mm, 1)
                pe.wait_ge(q_ready, B * h + B)
                for j in range(ST):
                    pe.wait_ge(s_abs, ST * h + max(j - 1, 0))
                    for b in range(B):
                        mm = pe.matmul(ps[:, 4 + j % 2, 0:S - P * j], ctxT[:, b * S + j * P:b * S + (j + 1) * P],
                                       q_sb[:, b, P * j:S], start=(b == 0), stop=(b == B - 1))
                    mm.then_inc(s_mm, 1)
                pe.wait_ge(v_ready, ST * h + ST)
                for i in range(ST):
                    pe.wait_ge(at_ready, ST * h + i + 1)
                    pe.wait_ge(o_ready, ST * h + max(i - 1, 0))
                    for j in range(ST):
                        a = at_sb[:, AT_OFF[j] + (i - j) * P:AT_OFF[j] + (i - j + 1) * P] if j <= i else ones
                        mm = pe.matmul(ps[:, 6 + i % 2, :], a, v_sb[:, j, :], start=(j == 0), stop=(j == ST - 1))
                    mm.then_inc(o_mm, 1)

            for h in range(H):
                head(h, h % 2, h // 2)

            pe.wait_ge(o_ready, ST * H)
            pe.wait_ge(w3_loaded, 48)

            def tr_a(t, p, half):
                pe.wait_ge(gated, t + 1)
                if type(t) is not int or t >= 2:
                    pe.wait_ge(a_xT, t - 1)
                transposes(ps[:, p, :], gin[:, p, :], KT, a_tr)

            def proj(t, p, half):
                pe.wait_ge(a_xT, t + 1)
                if type(t) is not int or t >= 2:
                    pe.wait_ge(x1_ready, t - 1)
                for k in range(KT):
                    mm = pe.matmul(ps[:, 2 + p, :], xT[:, p, k, :], wo_sb[:, k, :], start=(k == 0), stop=(k == KT - 1))
                mm.then_inc(a_mm, 1)

            def tr_b(t, p, half):
                pe.wait_ge(xn_ready, t + 1)
                if type(t) is not int or t >= 2:
                    pe.wait_ge(b_xT, t - 1)
                transposes(ps[:, 4 + p, :], xr[:, p, :], KT, b_tr)

            def router(t, p, half):
                pe.wait_ge(b_xT, t + 1)
                if type(t) is not int or t >= 2:
                    pe.wait_ge(r_ready, t - 1)
                for k in range(KT):
                    mm = pe.matmul(ps[:, 6 + p, 0:E], xT2[:, p, k, :], wr_sb[:, k, :], start=(k == 0), stop=(k == KT - 1))
                mm.then_inc(r_mm, 1)

            pipeline(pe, NT, [(1, tr_a), (0, proj), (-1, tr_b), (-2, router)])

            def route(t, r, turn):
                if type(t) is not int or t != 1:
                    return
                pe.wait_ge(rt_sel, 1)
                pe.wait_ge(cbf_ready, 1)
                pe.matmul(ps[:, 7, 0:NT * E], cbf[:, 0, :], sel[:, :], start=True, stop=False, skip_group_check=True)
                for d in range(1, NT):
                    pe.matmul(ps[:, 7, d * E:NT * E], cbf[:, 1, :], sel[:, 0:(NT - d) * E], start=False, stop=(d == NT - 1), skip_group_check=True)
                for i in range(NT):
                    mm = pe.matmul(ps[:, 7, NT * E:(NT + 1) * E], cbf[:, 1, :], sel[:, i * E:(i + 1) * E], start=(i == 0), stop=(i == NT - 1))
                mm.then_inc(rt_mm, 1)

            def tr_x(base):
                def fn(t, r, turn):
                    p = r % 2
                    pe.wait_ge(xg_loaded[r], 16 * (base // XG + turn + 1))
                    if base or type(t) is not int or t >= 2:
                        pe.wait_ge(x_lo, base + t - 1)
                    transposes(ps[:, p, :], xg[:, r, :], KT, x_tr)
                return fn

            def up(base, which):
                def fn(t, r, turn):
                    p = r % 2
                    a, need = which(t, 1 + (r + 1) % XG)
                    pe.wait_ge(x_lo, base + t + 1)
                    pe.wait_ge(h_ready, base + t)
                    pe.wait_ge(w13_ready, need)
                    for m in range(2):
                        for k in range(KT):
                            c = (2 * k + m) * INTER
                            xh, xl = xhi[:, p, k * P:(k + 1) * P], xlo[:, p, k * P:(k + 1) * P]
                            wh, wl = whi[:, a, c:c + INTER], wlo[:, a, c:c + INTER]
                            pe.matmul(ps[:, 2 + m, 0:INTER], xh, wh, start=(k == 0), stop=False)
                            pe.matmul(ps[:, 2 + m, 0:INTER], xh, wl, start=False, stop=False)
                            mm = pe.matmul(ps[:, 2 + m, 0:INTER], xl, wh, start=False, stop=(k == KT - 1))
                    mm.then_inc(mm1, 1)
                return fn

            def down(base, which):
                def fn(t, r, turn):
                    p = r % 2
                    a, need = which(t, (r + 2) % XG)
                    pe.wait_ge(h_lo, base + t + 1)
                    pe.wait_ge(w2_ready, need)
                    pe.wait_ge(y_out, base + t + 1)
                    for k in range(IC):
                        c = W13 + k * D
                        hh, hl = hhi[:, k * P:(k + 1) * P], hlo[:, k * P:(k + 1) * P]
                        wh, wl = whi[:, a, c:c + D], wlo[:, a, c:c + D]
                        pe.matmul(ps[:, 5 + p, :], hh, wh, start=(k == 0), stop=False)
                        pe.matmul(ps[:, 5 + p, :], hh, wl, start=False, stop=False)
                        mm = pe.matmul(ps[:, 5 + p, :], hl, wh, start=False, stop=(k == IC - 1))
                    mm.then_inc(mm2, 1)
                return fn

            def tr_h(base):
                def fn(t, p, half):
                    pe.wait_ge(h_ready, base + t + 1)
                    pe.wait_ge(h_lo, base + t)
                    transposes(ps[:, 4, :], hx[:, :], IC, h_tr)
                return fn

            words = []

            def load_words(j):
                words[:] = [pe.value_load(packed[0:1, bass.ds(2 * j + i, 1)], min_val=0, max_val=32 ** 3 - 1) for i in range(2)]

            def routed(t, entry):
                if type(t) is int:
                    need = pe.value_load(order[0:1, t:t + 1], min_val=2, max_val=E + 1)
                else:
                    i = min(entry // 2, 1)
                    need = words[i] // 32 ** (entry - 2 * i) % 32
                return bass.ds((need + 1) % 2, 1), need

            def phase(base, tiles, which, each_pass=None):
                extra = [(0, route)] if base == 0 else []
                pipeline(pe, tiles, [(0, up(base, which))] + extra + [(1, tr_x(base)), (-1, down(base, which)), (0, tr_h(base))],
                         ring=XG, each_pass=each_pass)

            pe.wait_ge(h_pad, 1)
            pe.wait_ge(r_ready, NT)
            phase(0, NT, lambda t, place: (0, 1))
            pe.wait_ge(rt_done, 1)
            phase(NT, NR, routed, load_words)
            phase(NT + NR, NT, lambda t, place: (1, NW))

        @block.vector
        def _(dve):
            def norm_1(t, r, turn):
                p = r % 2
                hold(dve, x_loaded[r], 16 * (turn + 1))
                dve.bn_stats(st1[:, p, :], xq[:, r, :]).then_inc(s1_stats, 1)
                hold(dve, s1_stats, t + 1)
                dve.bn_aggr(mv1[:, p, :], st1[:, p, :]).then_inc(s1_aggr, 1)
                dve.wait_ge(s1_std, t + 1)
                dve.reciprocal(sd1[:, p, 1:2], sd1[:, p, 0:1]).then_inc(s1_rstd, 1)
                dve.wait_ge(s1_rstd, t + 1)
                dve.tensor_scalar(xq[:, r, :], xq[:, r, :], mv1[:, p, 0:1], sd1[:, p, 1:2], ALU.subtract, ALU.mult).then_inc(s1_xn, 1)

            def keep_1(t, r, turn):
                p = r % 2
                dve.wait_ge(s1_xT, t + 1)
                dve.tensor_copy(xnT[:, :, bass.ds(t * P, P)], xT[:, p, :, :]).then_inc(s1_xnT, 1)

            pipeline(dve, NT, [(2, norm_1), (0, keep_1)], ring=XR)

            dve.wait_ge(qdec_loaded, 16)

            def head(h, p, half):
                dve.wait_ge(g_mm, h + 1)
                dve.wait_ge(q_mm, B * h)
                dve.tensor_copy(g_sb[:, :], ps[:, 0, 0:HD]).then_inc(g_ready, 1)
                dve.wait_ge(s_mm, ST * h)
                for b in range(B):
                    dve.wait_ge(q_mm, B * h + b + 1)
                    dve.tensor_tensor(q_sb[:, b:b + 1, :], ps[:, 2 + b % 2:3 + b % 2, :], qdec[:, bass.ds(h, 1), :], ALU.mult).then_inc(q_ready, 1)
                for j in range(ST):
                    dve.wait_ge(s_abs, ST * h + j + 1)
                    blk = at_sb[:, AT_OFF[j]:AT_OFF[j] + S - P * j]
                    dve.tensor_scalar(blk, blk, 1.0, None, ALU.max).then_inc(at_max, 1)
                for i in range(ST):
                    dve.wait_ge(o_ready, ST * h + i + 1)
                    for b in range(B):
                        t = b * ST + i
                        st = dve.bn_stats(st3[:, t, bass.ds(h, 1), :], o_sb[:, t, bass.ds(h * HD, HD)])
                st.then_inc(o_stats, 1)

            for h in range(H):
                head(h, h % 2, h // 2)

            dve.wait_ge(o_stats, H)
            for t in range(NT):
                dve.bn_aggr(mv3[:, t, :], st3[:, t, :, :]).then_inc(o_aggr, 1)
            dve.wait_ge(o_std, 1)
            dve.reciprocal(sd3[:, 1, :], sd3[:, 0, :]).then_inc(o_rstd, 1)
            dve.wait_ge(o_rstd, 1)
            dve.wait_ge(w3_loaded, 48)

            def first_low(t, p, half):
                dve.wait_ge(first_hi, t + 1)
                at = bass.ds(t * PIECE, PIECE)
                dve.tensor_tensor(wlo_all[:, at], raw_all[:, at], whi_all[:, at].bitcast(F32), ALU.subtract).then_inc(first_lo, 1)

            def norm_o(t, p, half):
                dve.tensor_scalar(o_sb[:, bass.ds(t, 1), :], o_sb[:, bass.ds(t, 1), :], mv3[:, bass.ds(t, 1), 0],
                                  sd3[:, 1, bass.ds(t, 1)], ALU.subtract, ALU.mult).then_inc(o_normed, 1)

            def gate_o(t, p, half):
                dve.wait_ge(o_beta, t + 1)
                dve.wait_ge(gate_loaded[p], 16 * (half + 1))
                dve.tensor_tensor(gin[:, p:p + 1, :], gin[:, p:p + 1, :], o_sb[:, bass.ds(t, 1), :], ALU.mult).then_inc(gated, 1)

            def norm_x1(t, p, half):
                dve.wait_ge(a_mm, t + 1)
                dve.wait_ge(x3_loaded[p], 16 * (half + 1))
                dve.tensor_tensor(x1[:, bass.ds(t, 1), :], ps[:, 2 + p:3 + p, :], xin[:, p:p + 1, :], ALU.add).then_inc(x1_ready, 1)
                hold(dve, x1_ready, t + 1)
                dve.bn_stats(st1[:, p, :], x1[:, bass.ds(t, 1), :]).then_inc(l_stats, 1)
                hold(dve, l_stats, t + 1)
                dve.bn_aggr(mv1[:, p, :], st1[:, p, :]).then_inc(l_aggr, 1)
                dve.wait_ge(l_std, t + 1)
                dve.reciprocal(sd1[:, p, 1:2], sd1[:, p, 0:1]).then_inc(l_rstd, 1)
                dve.wait_ge(l_rstd, t + 1)
                if type(t) is not int or t >= 2:
                    dve.wait_ge(b_tr, t - 1)
                    dve.wait_ge(xn_stored[p], 16 * half)
                dve.tensor_scalar(xr[:, p:p + 1, :], x1[:, bass.ds(t, 1), :], mv1[:, p, 0:1], sd1[:, p, 1:2],
                                  ALU.subtract, ALU.mult).then_inc(xn_ready, 1)

            def keep_logits(t, p, half):
                dve.wait_ge(r_mm, t + 1)
                dve.tensor_copy(logits[:, bass.ds(t, 1), :], ps[:, 6 + p:7 + p, 0:E]).then_inc(r_ready, 1)

            pipeline(dve, NT, [(3, norm_o), (2, gate_o), (0, norm_x1), (-1, first_low), (-2, keep_logits)])

            dve.wait_ge(first_lo, NT)
            dve.sem_inc(w13_ready, 2)
            dve.sem_inc(w2_ready, 2)

            steps = [0]

            def step(ins):
                steps[0] += 1
                ins.then_inc(rt, 1)
                dve.wait_ge(rt, steps[0])

            dve.wait_ge(r_ready, NT)
            for p in range(2):
                dve.wait_ge(xn_stored[p], 16 * (NT // 2))
            dve.memset(hx[:, :], 0.0).then_inc(h_pad, 1)
            step(dve.tensor_reduce(rmax[:, 0, :], logits[:, :, :], AX, ALU.max))
            step(dve.tensor_tensor(score[:, :, :], logits[:, :, :], rmax[:, 0, :, None].to_broadcast([P, NT, E]), ALU.subtract))
            def h_mult(base):
                def fn(t, p, half):
                    dve.wait_ge(silu, base + t + 1)
                    dve.wait_ge(h_tr, base + t)
                    dve.tensor_tensor(hx[:, 0:INTER], ps[:, 3, 0:INTER], sg[:, :], ALU.mult).then_inc(h_ready, 1)
                return fn

            def x_low(base):
                def fn(t, r, turn):
                    p = r % 2
                    dve.wait_ge(x_hi, base + t + 1)
                    dve.tensor_tensor(xlo[:, p, :], ps[:, p, :], xhi[:, p, :].bitcast(F32), ALU.subtract).then_inc(x_lo, 1)
                return fn

            def h_low(base):
                def fn(t, p, half):
                    dve.wait_ge(h_hi, base + t + 1)
                    dve.tensor_tensor(hlo[:, :], ps[:, 4, 0:IC * P], hhi[:, :].bitcast(F32), ALU.subtract).then_inc(h_lo, 1)
                return fn

            def add_shared(base):
              def fn(t, r, turn):
                p = r % 2
                dve.wait_ge(mm2, base + t + 1)
                dve.tensor_tensor(x1[:, bass.ds(t, 1), :], x1[:, bass.ds(t, 1), :], ps[:, 5 + p:6 + p, :], ALU.add).then_inc(y_out, 1)
              return fn

            mine = gsc[:, :, :, None].to_broadcast([P, NT, G, G])
            other = gsc[:, :, None, :].to_broadcast([P, NT, G, G])
            beats = gcmp[:, 0, :, :]
            ties = gcmp[:, 1, :, :]
            hot = onehot[:, :, :].rearrange("p t (k e) -> p t k e", k=TOPK)
            tc = tcmp[:, :].rearrange("p (a b) -> p a b", a=E)

            def r_scores():
                dve.wait_ge(rt_exp, 1)
                step(dve.tensor_reduce(rmax[:, 0, :], score[:, :, :], AX, ALU.add))
                step(dve.reciprocal(rmax[:, 1, :], rmax[:, 0, :]))
                step(dve.tensor_tensor(score[:, :, :], score[:, :, :], rmax[:, 1, :, None].to_broadcast([P, NT, E]), ALU.mult))
                step(dve.tensor_reduce(gsc[:, :, :], score[:, :, :].rearrange("p t (g e) -> p (t g) e", g=G), AX, ALU.max))
                step(dve.tensor_tensor(beats.rearrange("p t (g o) -> p t g o", g=G), other, mine, ALU.is_gt))
                step(dve.tensor_tensor(ties.rearrange("p t (g o) -> p t g o", g=G), other, mine, ALU.is_equal))

            def r_groups():
                step(dve.tensor_tensor(ties, ties, const[:, None, C_LG:C_LG + G * G].to_broadcast([P, NT, G * G]), ALU.mult))
                step(dve.tensor_tensor(beats, beats, ties, ALU.add))
                step(dve.tensor_reduce(gkeep[:, :, :], beats.rearrange("p t (g o) -> p (t g) o", g=G), AX, ALU.add))
                step(dve.tensor_scalar(gkeep[:, :, :], gkeep[:, :, :], TOPG - 0.5, -2.0, ALU.is_gt, ALU.mult))
                step(dve.tensor_tensor(masked[:, :, :].rearrange("p t (g e) -> p (t g) e", g=G),
                                       score[:, :, :].rearrange("p t (g e) -> p (t g) e", g=G),
                                       gkeep[:, :, :].rearrange("p t g -> p (t g)")[:, :, None].to_broadcast([P, NT * G, EG]), ALU.add))
                for t in range(NT):
                    last = dve.max(top8[:, t, :], masked[:, t, :])
                step(last)

            def r_experts():
                for t in range(NT):
                    last = dve.max_index(top8i[:, t, :], top8[:, t, :], masked[:, t, :])
                step(last)
                step(dve.tensor_copy(top8f[:, :, :], top8i[:, :, :]))
                step(dve.tensor_tensor(hot, top8f[:, :, 0:TOPK, None].to_broadcast([P, NT, TOPK, E]),
                                       const[:, None, None, C_IOTA:C_IOTA + E].to_broadcast([P, NT, TOPK, E]), ALU.is_equal))
                step(dve.tensor_reduce(self32[:, :, :], onehot[:, :, :].rearrange("p t (k e) -> p t e k", k=TOPK), AX, ALU.add))
                dve.tensor_copy(sel[:, :], self32[:, :, :].rearrange("p t e -> p (t e)")).then_inc(rt_sel, 1)

            def r_places():
                dve.wait_ge(rt_mm, 1)
                step(dve.tensor_copy(ntile[:, 1, :], ps[:, 7, NT * E:(NT + 1) * E]))
                step(dve.tensor_tensor(tc, ntile[:, 1, :, None].to_broadcast([P, E, E]),
                                       const[:, None, C_CAP:C_CAP + E].to_broadcast([P, E, E]), ALU.is_gt))
                step(dve.tensor_reduce(ntile[:, 0, :], tc, AX, ALU.add))
                step(dve.tensor_tensor(tc, ntile[:, 0, None, :].to_broadcast([P, E, E]),
                                       const[:, C_LT:C_LT + E * E].rearrange("p (a b) -> p a b", a=E), ALU.mult))
                step(dve.tensor_reduce(ntile[:, 1, :], tc, AX, ALU.add))
                step(dve.scalar_tensor_tensor(slot[:, :].rearrange("p (t e) -> p t e", t=NT), ntile[:, 1, None, :].to_broadcast([P, NT, E]),
                                              float(P), ps[:, 7, 0:NT * E].rearrange("p (t e) -> p t e", t=NT), ALU.mult, ALU.add))

            def r_slots():
                step(dve.tensor_tensor(pick[:, :, :].rearrange("p t (k e) -> p t k e", k=TOPK), hot,
                                       slot[:, :].rearrange("p (t e) -> p t e", t=NT)[:, :, None, :].to_broadcast([P, NT, TOPK, E]), ALU.mult))
                step(dve.tensor_reduce(slotf[:, :], pick[:, :, :].rearrange("p t (k e) -> p (t k) e", k=TOPK), AX, ALU.add))
                dve.tensor_copy(sloti[:, :], slotf[:, :]).then_inc(rt_slots, 1)

            def r_tables():
                step(dve.tensor_tensor(ntile[0:1, 0, :], ntile[0:1, 0, :], ntile[0:1, 1, :], ALU.add))
                step(dve.tensor_tensor(ecmp[:, :, :], ntile[0:1, 0, None, :].to_broadcast([1, NR, E]),
                                       const[0:1, C_TILE:C_TILE + NR, None].to_broadcast([1, NR, E]), ALU.is_le))
                step(dve.tensor_reduce(tabf[:, 0:NR], ecmp[:, :, :], AX, ALU.add))
                step(dve.tensor_scalar(tabf[:, 0:NR], tabf[:, 0:NR], float(E - 1), 2.0, ALU.min, ALU.add))
                step(dve.tensor_scalar(tabf[:, NR:NR + E], ntile[0:1, 1, :], float(NT), None, ALU.add))
                step(dve.tensor_copy(order[:, :], tabf[:, :]))
                n = (NR - 4) // 2
                entry = [tabf[:, i:i + 2 * n - 1:2] for i in (2, 3, 4)]
                step(dve.scalar_tensor_tensor(packf[:, :], entry[2], 32.0, entry[1], ALU.mult, ALU.add))
                step(dve.scalar_tensor_tensor(packf[:, :], packf[:, :], 32.0, entry[0], ALU.mult, ALU.add))
                dve.tensor_copy(packed[:, :], packf[:, :]).then_inc(rt_done, 1)

            def route(t, r, turn):
                if type(t) is int and t < 3:
                    for part in ((r_experts,), (r_places, r_slots), (r_tables,))[t]:
                        part()

            def combine(t, r, turn):
                p = r % 2
                dve.wait_ge(y_out, 2 + NT + NR + t + 1)
                if type(t) is not int or t >= 2:
                    dve.wait_ge(out_stored[p], 16 * (GR // 2 * turn + r // 2))
                dve.wait_ge(gathered[r], 16 * TOPK * (turn + 1))
                for k in range(TOPK):
                    if k:
                        dve.wait_ge(comb, TOPK * t + k)
                    so_far = osb[:, p:p + 1, :] if k else x1[:, bass.ds(t, 1), :]
                    dve.scalar_tensor_tensor(osb[:, p:p + 1, :], gath[:, r, k:k + 1, :], top8[:, bass.ds(t, 1), k], so_far,
                                             ALU.mult, ALU.add).then_inc(comb, 1)

            r_scores()
            r_groups()
            pipeline(dve, NT, [(0, h_mult(0)), (1, x_low(0)), (-1, add_shared(0)), (0, h_low(0)), (0, route)])
            pipeline(dve, NR, [(0, h_mult(NT)), (1, x_low(NT)), (0, h_low(NT))])
            pipeline(dve, NT, [(0, h_mult(NT + NR)), (1, x_low(NT + NR)), (-1, add_shared(NT + NR)), (0, h_low(NT + NR)), (-4, combine)], ring=GR)


def constants():
    import numpy as np
    c = np.zeros((P, C_ALL), np.float32)
    r = np.arange(P)
    c[:, C_ID:C_ID + P] = np.eye(P)
    c[:, C_UP:C_UP + P] = r[:, None] < r[None, :]
    c[:, C_ONE:C_ONE + P] = 1.0
    e = np.arange(E)
    c[:, C_IOTA:C_IOTA + E] = e
    c[:, C_CAP:C_CAP + E] = P * e
    c[:, C_LT:C_LT + E * E] = (e[None, :] < e[:, None]).reshape(-1)
    g = np.arange(G)
    c[:, C_LG:C_LG + G * G] = (g[None, :] < g[:, None]).reshape(-1)
    c[:, C_TILE:C_TILE + NR] = np.arange(NR)
    c[:, C_EPS] = LN_EPS
    c[:, C_EPS + 1] = GN_EPS
    gam = 1.0 - 2.0 ** (-5.0 - np.arange(H, dtype=np.float64))
    query = gam[:, None] ** -np.arange(S, dtype=np.float64)[None, :]
    key = 1.0 / query / np.sqrt(np.cumsum(query, axis=1)) / np.sqrt(float(HD))
    c[:, C_KDEC:C_KDEC + H * ST] = key.reshape(H * ST, P).T
    return c, query.astype(np.float32)


def kernel(**inputs):
    import numpy as np
    import concourse.bacc as bacc
    from concourse.bass_utils import run_bass_kernel_spmd as run

    x = np.ascontiguousarray(inputs["x"]).reshape(TOK, D)
    ctxT = np.ascontiguousarray(inputs["ctx_2048"]).reshape(TOK, D).T.reshape(H, HD, TOK)
    wh = np.ascontiguousarray(inputs["L0_xattn_Wh"])
    heads = np.concatenate([ctxT, wh, wh.transpose(0, 2, 1)], axis=2)
    gn = np.stack([inputs["L0_xattn_gn_gamma"], inputs["L0_xattn_gn_beta"]])

    def pieces(w1, w3, w2):
        up = np.stack([w1.T.reshape(KT, P, INTER), w3.T.reshape(KT, P, INTER)], axis=2)
        down = np.zeros((IC * P, D), w2.dtype)
        down[:INTER] = w2.T
        return np.concatenate([up.transpose(1, 0, 2, 3).reshape(P, W13),
                               down.reshape(IC, P, D).transpose(1, 0, 2).reshape(P, IC * D)], axis=1)

    w1, w3, w2 = (np.asarray(inputs[f"L0_ffn_W{n}"]) for n in (1, 3, 2))
    s1, s3, s2 = (np.asarray(inputs[f"L0_ffn_Ws{n}"]) for n in (1, 3, 2))
    shared = [pieces(s1[i * INTER:(i + 1) * INTER], s3[i * INTER:(i + 1) * INTER], s2[:, i * INTER:(i + 1) * INTER])
              for i in range(N_SHARED)]
    wexp = np.stack([shared[0]] + [pieces(w1[e], w3[e], w2[e]) for e in range(E)] + [shared[1]])
    tables, qdecay = constants()

    arrays = {"x_in": x, "heads_in": heads, "wg_in": inputs["L0_xattn_wg_w"], "wo_in": inputs["L0_xattn_wo_w"],
              "gn_in": gn, "router_in": np.asarray(inputs["L0_ffn_Wg"]).T, "wexp_in": wexp,
              "tables_in": tables, "qdecay_in": qdecay}
    arrays = {n: np.ascontiguousarray(a) for n, a in arrays.items()}
    nc = bacc.Bacc("TRN2", target_bir_lowering=False, num_devices=1)
    aps = [nc.dram_tensor(n, a.shape, mybir.dt.from_np(a.dtype), kind="ExternalInput").ap() for n, a in arrays.items()]
    out = nc.dram_tensor("y_out", (B, S, D), F32, kind="ExternalOutput").ap()
    xattn_moe(nc, *aps, out.rearrange("b s d -> (b s) d"))
    r = run(nc, [arrays], core_ids=[0])
    return r.results[0]["y_out"]
```
